# Optimizing a Trainium2 kernel written in Bass

```python
import numpy as np
import jax
import jax.numpy as jnp

def _softmax(x, axis=-1):
    return jax.nn.softmax(x, axis=axis)

def _gelu(x):
    return jax.nn.gelu(x, approximate=True)

def _silu(x):
    return jax.nn.silu(x)

def _sigmoid(x):
    return jax.nn.sigmoid(x)

def _layernorm(x, axis=-1, eps=1e-05):
    m = jnp.mean(x, axis=axis, keepdims=True)
    v = jnp.var(x, axis=axis, keepdims=True)
    return (x - m) / jnp.sqrt(v + eps)

def _scatter_add(tgt, idx, src, axis=0):
    return tgt.at[idx].add(src)

def _segment_sum(src, seg, n):
    return jax.ops.segment_sum(src, seg, n)
kernel_name = 'mk_adj_resnorm_d2_adj_r2_476b26'

def setup_inputs(seed: int=0):
    np.random.seed(seed)
    _w = jnp.asarray

    def _rec_inputs():
        import jax
        import jax.numpy as jnp
        _gk = jax.random.key(seed)
        x = -0.0002928 + 1 * jax.random.normal(jax.random.fold_in(_gk, 1), (16, 512, 256), jnp.float32)
        _a = jax.random.bernoulli(jax.random.fold_in(_gk, 2), 0.0078125, (16, 512, 512))
        _a = jnp.logical_or(_a, jnp.swapaxes(_a, -1, -2))
        _a = jnp.logical_or(_a, jnp.eye(512, dtype=bool))
        _af = _a.astype(jnp.float32)
        _af = _af * jax.random.uniform(jax.random.fold_in(_gk, 3), (16, 512, 512), jnp.float32, 0.05, 1)
        adj = _af
        return (x, adj)
    x, adj = _rec_inputs()

    def _L0_gnn_setup():
        import jax, jax.numpy as jnp
        import numpy as np
        B, N, DIN, DOUT, K = (4, 1024, 256, 256, 3)
        key = jax.random.key(seed)
        ks = jax.random.split(key, 8)
        X = jax.random.normal(ks[0], (B, N, DIN), dtype=jnp.float32)
        A = jax.random.uniform(ks[1], (B, N, N), dtype=jnp.float32)
        Wv = jax.random.normal(ks[2], (DIN, DOUT), dtype=jnp.float32) * 0.02
        bv = jax.random.normal(ks[3], (DOUT,), dtype=jnp.float32) * 0.02
        aw = jax.random.normal(ks[4], (2 * DOUT, 1), dtype=jnp.float32) * 0.05
        ab = jax.random.normal(ks[5], (1,), dtype=jnp.float32) * 0.05
        Wk = jax.random.normal(ks[6], (K, DIN, DOUT), dtype=jnp.float32) * 0.02
        bk = jax.random.normal(ks[7], (K, DOUT), dtype=jnp.float32) * 0.02
        return {'X': X, 'A': A, 'Wv': Wv, 'bv': bv, 'aw': aw, 'ab': ab, 'Wk': Wk, 'bk': bk}
    _L0_gnn_all = _L0_gnn_setup()
    _L0_gnn_in = {k: v for k, v in _L0_gnn_all.items() if k in ('Wv', 'bv', 'aw', 'ab', 'Wk', 'bk')}
    del _L0_gnn_all

    def _L1_gnn_setup():
        import jax, jax.numpy as jnp
        import numpy as np
        EPS_LN = 1e-05

        def hypergraph_conv(x, adj, W, b):
            N, C, _ = adj.shape
            H = (adj != 0).astype(x.dtype)
            w = adj.reshape(N, -1)[:, :C]
            xw = jnp.einsum('ncd,hd->nch', x, W)
            Dn = jnp.einsum('nce,ne->nc', H, w)
            Dn = jnp.where(Dn > 0, 1.0 / Dn, 0.0)
            Be = H.sum(axis=1)
            Be = jnp.where(Be > 0, 1.0 / Be, 0.0)
            m = Be[:, :, None] * jnp.einsum('nce,nch->neh', H, xw)
            out = Dn[:, :, None] * jnp.einsum('nce,neh->nch', H, m)
            return out + b

        def layer_norm(x, g, b):
            mu = jnp.mean(x, axis=-1, keepdims=True)
            var = jnp.var(x, axis=-1, keepdims=True)
            return (x - mu) * jax.lax.rsqrt(var + EPS_LN) * g + b
        key = jax.random.key(seed)
        ks = jax.random.split(key, 4)
        N, C, Din, Dh, Dout = (16, 512, 256, 512, 256)
        x = jax.random.normal(ks[0], (N, C, Din), dtype=jnp.float32)
        adj = jax.random.uniform(ks[1], (N, C, C), dtype=jnp.float32, minval=0.1, maxval=1.0)
        W1 = jax.random.normal(ks[2], (Dh, Din), dtype=jnp.float32) * (1.0 / np.sqrt(Din))
        b1 = jnp.zeros((Dh,), dtype=jnp.float32)
        gamma = jnp.ones((Dh,), dtype=jnp.float32)
        beta = jnp.zeros((Dh,), dtype=jnp.float32)
        W2 = jax.random.normal(ks[3], (Dout, Dh), dtype=jnp.float32) * (1.0 / np.sqrt(Dh))
        b2 = jnp.zeros((Dout,), dtype=jnp.float32)
        return {'x': x, 'adj': adj, 'W1': W1, 'b1': b1, 'gamma': gamma, 'beta': beta, 'W2': W2, 'b2': b2}
    _L1_gnn_all = _L1_gnn_setup()
    _L1_gnn_in = {k: v for k, v in _L1_gnn_all.items() if k in ('W1', 'b1', 'gamma', 'beta', 'W2', 'b2')}
    del _L1_gnn_all
    return {'x': x, 'adj': adj, 'L0_gnn_Wv': _L0_gnn_in['Wv'], 'L0_gnn_bv': _L0_gnn_in['bv'], 'L0_gnn_aw': _L0_gnn_in['aw'], 'L0_gnn_ab': _L0_gnn_in['ab'], 'L0_gnn_Wk': _L0_gnn_in['Wk'], 'L0_gnn_bk': _L0_gnn_in['bk'], 'L1_gnn_W1': _L1_gnn_in['W1'], 'L1_gnn_b1': _L1_gnn_in['b1'], 'L1_gnn_gamma': _L1_gnn_in['gamma'], 'L1_gnn_beta': _L1_gnn_in['beta'], 'L1_gnn_W2': _L1_gnn_in['W2'], 'L1_gnn_b2': _L1_gnn_in['b2']}

def reference(x, adj, L0_gnn_Wv, L0_gnn_bv, L0_gnn_aw, L0_gnn_ab, L0_gnn_Wk, L0_gnn_bk, L1_gnn_W1, L1_gnn_b1, L1_gnn_gamma, L1_gnn_beta, L1_gnn_W2, L1_gnn_b2):
    import jax
    import jax.numpy as jnp

    def _L0_gnn_ref(X, A, Wv, bv, aw, ab, Wk, bk):
        import jax, jax.numpy as jnp
        import numpy as np
        B, N, DIN, DOUT, K = (4, 1024, 256, 256, 3)
        d = Wv.shape[1]
        Xw = X @ Wv + bv
        sj = Xw @ aw[:d, 0]
        si = Xw @ aw[d:, 0]
        e = jax.nn.leaky_relu(sj[:, None, :] + si[:, :, None] + ab[0], negative_slope=0.2)
        alpha_matrix = A * jnp.exp(e)
        transition = alpha_matrix / (jnp.sum(alpha_matrix, axis=-1, keepdims=True) + 1e-12)
        H = jnp.zeros(X.shape[:-1] + (d,), dtype=X.dtype)
        Xk = X
        for k in range(Wk.shape[0]):
            H = H + Xk @ Wk[k] + bk[k]
            Xk = jnp.einsum('bij,bjd->bid', transition, Xk)
        return jax.nn.relu(H)

    def _L1_gnn_ref(x, adj, W1, b1, gamma, beta, W2, b2):
        import jax, jax.numpy as jnp
        import numpy as np
        EPS_LN = 1e-05

        def hypergraph_conv(x, adj, W, b):
            N, C, _ = adj.shape
            H = (adj != 0).astype(x.dtype)
            w = adj.reshape(N, -1)[:, :C]
            xw = jnp.einsum('ncd,hd->nch', x, W)
            Dn = jnp.einsum('nce,ne->nc', H, w)
            Dn = jnp.where(Dn > 0, 1.0 / Dn, 0.0)
            Be = H.sum(axis=1)
            Be = jnp.where(Be > 0, 1.0 / Be, 0.0)
            m = Be[:, :, None] * jnp.einsum('nce,nch->neh', H, xw)
            out = Dn[:, :, None] * jnp.einsum('nce,neh->nch', H, m)
            return out + b

        def layer_norm(x, g, b):
            mu = jnp.mean(x, axis=-1, keepdims=True)
            var = jnp.var(x, axis=-1, keepdims=True)
            return (x - mu) * jax.lax.rsqrt(var + EPS_LN) * g + b
        h = jax.nn.relu(hypergraph_conv(x, adj, W1, b1))
        h = layer_norm(h, gamma, beta)
        y = hypergraph_conv(h, adj, W2, b2)
        return y + x
    x = _layernorm(x + _L0_gnn_ref(x, adj, L0_gnn_Wv, L0_gnn_bv, L0_gnn_aw, L0_gnn_ab, L0_gnn_Wk, L0_gnn_bk), axis=-1)
    x = _layernorm(x + _L1_gnn_ref(x, adj, L1_gnn_W1, L1_gnn_b1, L1_gnn_gamma, L1_gnn_beta, L1_gnn_W2, L1_gnn_b2), axis=-1)
    return x

_drawn_inputs = setup_inputs


def setup_inputs(seed=0):
    import zlib

    import numpy as np

    out = dict(_drawn_inputs(seed))
    spreads = {'L1_gnn_b1': (0.0, 0.1),
     'L1_gnn_gamma': (1.0, 0.2),
     'L1_gnn_beta': (0.0, 0.1),
     'L1_gnn_b2': (0.0, 0.1)}
    factors = {'L0_gnn_Wv': 3.674, 'L0_gnn_bv': 22.336, 'L0_gnn_aw': 3.733}
    for name, (base, spread) in spreads.items():
        noise = np.random.default_rng([zlib.crc32(name.encode()), seed]).standard_normal(out[name].shape)
        drawn = base * np.exp(spread * noise) if base else spread * noise
        out[name] = jnp.asarray(drawn.astype(out[name].dtype))
    for name, factor in factors.items():
        out[name] = (out[name] * factor).astype(out[name].dtype)
    return out
```

```python
from contextlib import ExitStack

import concourse.bass as bass
from concourse import mybir

P = 128
F32 = mybir.dt.float32
F32R = mybir.dt.float32r
ALU = mybir.AluOpType
ACT = mybir.ActivationFunctionType
AX_X = mybir.AxisListType.X
DMA = 16


class Count:

    def __init__(self, sem, per, unit=1):
        self.sem, self.per, self.unit = sem, per, unit

    def value(self, n, k):
        return (n * self.per + k) * self.unit


class Graph:

    def __init__(self, n, parity):
        self.n, self.parity = n, parity


def wait(engine, count, n, k):
    value = count.value(n, k)
    if isinstance(value, int) and value <= 0:
        return
    engine.wait_ge(count.sem, value)


def gnn_resnorm(nc, x, adj, Wv, bv, aw, ab, Wk, bk, W1, b1, gamma, beta, W2, b2, out):
    G, N, D = x.shape
    HID = W1.shape[0]
    NB, DB, HB = N // P, D // P, HID // P
    EPS = 1e-5
    NEG = 0.2
    DA = D + 2
    LN_STEPS = 2 * NB + 2
    assert N == 512 and HID == 512 and D == 256 and G % 2 == 0

    with ExitStack() as ctx:
        def sb(name, shape, dt=F32):
            return ctx.enter_context(nc.sbuf_tensor(name, shape, dt))

        def sem(name):
            return ctx.enter_context(nc.semaphore(name))

        def per_graph(name, per, unit=1):
            return Count(sem(name), per, unit)

        ident = sb("ident", [P, P])
        wa_hi, wa_lo = (sb(f"wa_{s}", [P, DB, DA], F32R) for s in ("hi", "lo"))
        wb_hi, wb_lo = (sb(f"wb_{s}", [P, DB, 2 * D], F32R) for s in ("hi", "lo"))
        w1t_hi, w1t_lo = (sb(f"w1t_{s}", [P, DB, HID], F32R) for s in ("hi", "lo"))
        w2c_hi, w2c_lo = (sb(f"w2c_{s}", [P, HB, D], F32R) for s in ("hi", "lo"))
        score_const = sb("score_const", [P, 2])
        bk_row = sb("bk_row", [P, D])
        b1_row = sb("b1_row", [P, HID])
        b2_row = sb("b2_row", [P, D])
        bw_row = sb("bw_row", [P, D])
        minus_half = sb("minus_half", [P, NB])
        small = sb("small", [P, 16])

        x_in = [sb(f"x_in{i}", [P, NB, D]) for i in range(2)]
        adj_in = sb("adj_in", [P, NB, N])
        w_row = sb("w_row", [P, N])
        xt_hi, xt_lo = (sb(f"xt_{s}", [P, DB, N], F32R) for s in ("hi", "lo"))
        y2_hi = sb("y2_hi", [P, NB, DA], F32R)
        y2_lo = sb("y2_lo", [P, NB, D], F32R)
        y10 = sb("y10", [P, NB, 2 * D])
        scores = sb("scores", [P, NB, 2])
        score8, score2 = sb("score8", [P, NB]), sb("score2", [P, NB])
        si_rep = sb("si_rep", [P, NB, P])
        si_row, si_row2 = sb("si_row", [P, N]), sb("si_row2", [P, N])
        alpha = sb("alpha", [P, NB, N])
        al_hi, al_lo = (sb(f"al_{s}", [P, NB, N], F32R) for s in ("hi", "lo"))
        v_hi, v_lo = (sb(f"v_{s}", [P, NB, D], F32R) for s in ("hi", "lo"))
        rowsum, rowinv = sb("rowsum", [P, NB]), sb("rowinv", [P, NB])
        stats0, moments0 = sb("stats0", [P, NB, 6]), sb("moments0", [P, NB, 2])
        var0, rstd0 = sb("var0", [P, NB]), sb("rstd0", [P, NB])

        x1 = sb("x1", [P, NB, D])
        x1_hi = sb("x1_hi", [P, NB, DA], F32R)
        x1_lo = sb("x1_lo", [P, NB, D], F32R)
        x1_b2 = [sb(f"x1_b2_{i}", [P, NB, D]) for i in range(2)]
        inc = sb("inc", [P, NB, N], F32R)
        inc_t = [sb(f"inc_t{i}", [P, NB, N], F32R) for i in range(2)]
        deg = sb("deg", [P, 4, NB])
        dn = [sb(f"dn{i}", [P, NB]) for i in range(2)]
        masked = sb("masked", [P, N])

        be_count, be = sb("be_count", [P, NB]), sb("be", [P, NB])
        m_hi, m_lo = (sb(f"m_{s}", [P, NB, D], F32R) for s in ("hi", "lo"))
        ut_hi, ut_lo = (sb(f"ut_{s}", [P, DB, N], F32R) for s in ("hi", "lo"))
        h = sb("h", [P, NB, HID])
        stats1, moments1 = sb("stats1", [P, NB, 6]), sb("moments1", [P, NB, 2])
        var1, rstd1 = sb("var1", [P, NB]), sb("rstd1", [P, NB])
        ht_hi, ht_lo = (sb(f"ht_{s}", [P, HB, N], F32R) for s in ("hi", "lo"))
        hw = sb("hw", [P, NB, D])
        hw_hi = ut_hi[:, :, :].rearrange("p d (a c) -> p (d a) c", c=D)
        hw_lo = ut_lo[:, :, :].rearrange("p d (a c) -> p (d a) c", c=D)
        y = hw
        stats2, moments2 = sb("stats2", [P, NB, 6]), sb("moments2", [P, NB, 2])
        var2, rstd2 = sb("var2", [P, NB]), sb("rstd2", [P, NB])

        pb = [ctx.enter_context(nc.psum_tensor(f"pb{i}", [P, 512], F32)) for i in range(4)]
        pc = [ctx.enter_context(nc.psum_tensor(f"pc{i}", [P, 512], F32)) for i in range(4)]
        bank_xt = [pb[0], pb[1]]
        bank_a = [pb[2], pb[3], pb[0], pb[1]]
        bank_si = pb[2]
        bank_l0 = [pb[3], pb[0], pb[1], pb[2]]
        M_ORDER = (2, 3, 0, 1)
        bank_l1 = [pc[2], pc[3], pc[0], pc[1]]

        ident_done = sem("ident_done")
        score_in, wk_in, w1_in, w2_in, rows_in = (
            sem(s) for s in ("score_in", "wk_in", "w1_in", "w2_in", "rows_in"))
        set_dve = sem("set_dve")
        set_act = sem("set_act")
        set_pe = sem("set_pe")
        set_pool = sem("set_pool")
        x_loaded, adj_loaded, w_loaded = (
            per_graph(s, 1, DMA) for s in ("x_loaded", "adj_loaded", "w_loaded"))
        stored = per_graph("stored", 1, DMA)
        xt_ps, proj_a, si_ps, adj_t, proj_b, hop1, hop2 = (
            per_graph(s, k) for s, k in (("xt_ps", DB), ("proj_a", NB), ("si_ps", 1), ("adj_t", NB),
                                         ("proj_b", NB), ("hop1", NB), ("hop2", NB)))
        xt_hi_done, xt_lo_done = per_graph("xt_hi_done", DB), per_graph("xt_lo_done", DB)
        y2_hi_done, y2_lo_done = per_graph("y2_hi_done", NB), per_graph("y2_lo_done", NB)
        scores_done, score_cols, si_rep_done = (
            per_graph("scores_done", NB), per_graph("score_cols", 2), per_graph("si_rep_done", 1))
        si_rows = per_graph("si_rows", 2)
        inc_t_done = per_graph("inc_t_done", NB)
        lrelu_done, exp_done, alpha_done = (
            per_graph(s, NB) for s in ("lrelu_done", "exp_done", "alpha_done"))
        al_hi_done, al_lo_done = per_graph("al_hi_done", NB), per_graph("al_lo_done", NB)
        y10_done, bias_done = per_graph("y10_done", NB), per_graph("bias_done", 1)
        rowinv_done = per_graph("rowinv_done", 2 * NB)
        v_done, v_hi_done, v_lo_done = (
            per_graph("v_done", NB), per_graph("v_hi_done", 2), per_graph("v_lo_done", 2))
        hop2_read, res_done, ln0 = per_graph("hop2_read", NB), per_graph("res_done", NB), per_graph("ln0", LN_STEPS)
        rstd0_done = per_graph("rstd0_done", 1)
        x1_done, x1_twice, x1_hi_done, x1_lo_done, x1_b2_done = (
            per_graph("x1_done", NB), per_graph("x1_twice", 1), per_graph("x1_hi_done", 1), per_graph("x1_lo_done", 1),
            per_graph("x1_b2_done", 1))
        inc_done, dn_sum, dn_step = per_graph("inc_done", 1), per_graph("dn_sum", NB), per_graph("dn_step", 5)
        m_ps, ut_ps, z_ps, ht_ps, hw_ps, m2_ps, y_ps = (
            per_graph(s, k) for s, k in (("m_ps", NB), ("ut_ps", DB), ("z_ps", NB), ("ht_ps", HB),
                                         ("hw_ps", NB), ("m2_ps", NB), ("y_ps", NB)))
        be_done = per_graph("be_done", 2 * NB)
        m_hi_done, m_lo_done = per_graph("m_hi_done", NB), per_graph("m_lo_done", NB)
        ut_hi_done, ut_lo_done = per_graph("ut_hi_done", DB), per_graph("ut_lo_done", DB)
        z_done, h_done, ln1 = per_graph("z_done", NB), per_graph("h_done", NB), per_graph("ln1", LN_STEPS)
        rstd1_done = per_graph("rstd1_done", 1)
        ht_hi_done, ht_lo_done = per_graph("ht_hi_done", HB), per_graph("ht_lo_done", HB)
        hw_done, hw_hi_done, hw_lo_done = (
            per_graph("hw_done", NB), per_graph("hw_hi_done", NB), per_graph("hw_lo_done", NB))
        m2_hi_done, m2_lo_done = per_graph("m2_hi_done", NB), per_graph("m2_lo_done", NB)
        y_done, ln2, rstd2_done, out_done = (
            per_graph("y_done", NB), per_graph("ln2", LN_STEPS), per_graph("rstd2_done", 1),
            per_graph("out_done", NB))

        wa_f = alpha[:, 0:2, :].rearrange("p a n -> p (a n)")[:, 0:DB * DA].rearrange(
            "p (k c) -> p k c", c=DA)
        wb_f = alpha[:, 2:4, :]
        w1_f = y10[:, 0:2, :].rearrange("p a (b c) -> p (a b) c", c=D)
        w2_f = y10[:, 2:4, :]
        w2_g = hw[:, :, :].rearrange("p a c -> p (a c)").rearrange("p (o k) -> p o k", k=HID)
        wv_f = h[:, 0, :].rearrange("p (k c) -> p k c", c=D)
        aw_f = h[:, 1, :]
        bv_f = h[:, 2, 0:D]
        ab_f = h[:, 2, D:D + 1]
        gamma_f = h[:, 3, :]
        beta_f = x1[:, 0:2, :].rearrange("p a c -> p (a c)")
        bk_f = x1_b2[0][:, 0:3, :]
        bw_rep = si_rep[:, 0:2, :]

        def f32(ap):
            return ap.bitcast(F32)

        block = ctx.enter_context(nc.Block())

        def all_graphs(engine, pair):
            pair(None, Graph(0, 0))
            pair(Graph(0, 0), Graph(1, 1))
            with engine.Fori(0, (G - 2) // 2) as i:
                pair(Graph(i * 2 + 1, 1), Graph(i * 2 + 2, 0))
                pair(Graph(i * 2 + 2, 0), Graph(i * 2 + 3, 1))
            pair(Graph(G - 1, (G - 1) % 2), None)

        @block.sync
        def _(sp):
            def across(row):
                return row.partition_broadcast(P)

            sp.dma_start(wv_f, Wv.rearrange("(k p) c -> p k c", p=P)).then_inc(score_in, DMA)
            sp.dma_start(aw_f, across(aw.rearrange("a b -> (a b)"))).then_inc(score_in, DMA)
            sp.dma_start(bv_f, across(bv)).then_inc(score_in, DMA)
            sp.dma_start(ab_f, across(ab)).then_inc(score_in, DMA)

            def load_first(n, parity):
                sp.dma_start(x_in[parity][:, :, :],
                             x[bass.ds(n, 1), :, :].rearrange("g (r p) c -> p (g r) c", p=P)
                             ).then_inc(x_loaded.sem, DMA)

            def load_adj(n):
                sp.dma_start(adj_in[:, :, :],
                             adj[bass.ds(n, 1), :, :].rearrange("g (r p) c -> p (g r) c", p=P)
                             ).then_inc(adj_loaded.sem, DMA)
                sp.dma_start(w_row[:, :], adj[bass.ds(n, 1), 0:1, :].rearrange("g a c -> (g a c)")
                             .partition_broadcast(P)).then_inc(w_loaded.sem, DMA)

            load_first(0, 0)
            sp.dma_start(wa_f[:, :, 0:D], Wk[2].rearrange("(k p) c -> p k c", p=P)).then_inc(wk_in, DMA)
            sp.dma_start(wb_f[:, :, 0:D], Wk[1].rearrange("(k p) c -> p k c", p=P)).then_inc(wk_in, DMA)
            sp.dma_start(wb_f[:, :, D:2 * D], Wk[0].rearrange("(k p) c -> p k c", p=P)).then_inc(wk_in, DMA)
            load_adj(0)
            sp.dma_start(w1_f, W1.rearrange("(k p) c -> p k c", p=P)).then_inc(w1_in, DMA)
            sp.dma_start(w2_f, W2.rearrange("(k p) c -> p k c", p=P)).then_inc(w2_in, DMA)
            sp.dma_start(gamma_f, across(gamma)).then_inc(w2_in, DMA)
            sp.dma_start(beta_f, across(beta)).then_inc(w2_in, DMA)
            sp.dma_start(bk_f, across(bk.rearrange("a c -> (a c)")).rearrange("p (a c) -> p a c", c=D)
                         ).then_inc(rows_in, DMA)
            sp.dma_start(b1_row[:, :], across(b1)).then_inc(rows_in, DMA)
            sp.dma_start(b2_row[:, :], across(b2)).then_inc(rows_in, DMA)

            def pair(second, first):
                if first is not None and not (isinstance(first.n, int) and first.n == 0):
                    n = first.n
                    wait(sp, x_loaded, n - 1, 1)
                    wait(sp, res_done, n - 2, NB)
                    load_first(n, first.parity)
                    wait(sp, inc_done, n - 1, 1)
                    wait(sp, dn_sum, n - 1, NB)
                    load_adj(n)
                if second is not None:
                    n = second.n
                    wait(sp, out_done, n, NB)
                    sp.dma_start(out[bass.ds(n, 1), :, :].rearrange("g (r p) c -> p (g r) c", p=P),
                                 y[:, :, :]).then_inc(stored.sem, DMA)

            all_graphs(sp, pair)
            wait(sp, stored, G - 1, 1)

        @block.tensor
        def _(pe):
            def product(bank, terms, signal, width=None):
                for t, (left, right) in enumerate(terms):
                    last = nc.tensor.matmul(bank[:, 0:right.shape[-1]], left, right,
                                            start=(t == 0), stop=(t == len(terms) - 1))
                last.then_inc(signal, 1)

            def transposes(bank, blocks, signal):
                for t, block_in in enumerate(blocks):
                    last = nc.tensor.transpose(bank[:, t * P:(t + 1) * P], block_in, ident[:, :])
                last.then_inc(signal, 1)

            def cols(ap, k, b):
                return ap[:, k, b * P:(b + 1) * P]

            def transpose_x(g):
                xs = x_in[g.parity]
                wait(pe, x_loaded, g.n, 1)
                for k in range(DB):
                    wait(pe, hop2_read, g.n - 1, 2 + k)
                    transposes(bank_xt[k], [cols(xs, r, k) for r in range(NB)], xt_ps.sem)

            def project_a(g):
                wait(pe, xt_hi_done, g.n, DB)
                wait(pe, xt_lo_done, g.n, DB)
                for r in range(NB):
                    if r == 0:
                        wait(pe, hop2_read, g.n - 1, NB)
                    product(bank_a[r], [(cols(a, k, r), b[:, k, :]) for k in range(DB)
                                        for a, b in ((xt_hi, wa_hi), (xt_hi, wa_lo), (xt_lo, wa_hi))],
                            proj_a.sem)

            def transpose_si(g):
                wait(pe, si_rep_done, g.n, 1)
                wait(pe, y2_lo_done, g.n, 1)
                transposes(bank_si, [si_rep[:, r, :] for r in range(NB)], si_ps.sem)

            def transpose_adj(g):
                wait(pe, adj_loaded, g.n, 1)
                for j in range(NB):
                    if j < NB - 1:
                        wait(pe, y2_lo_done, g.n, j + 2)
                        wait(pe, scores_done, g.n, j + 2)
                    else:
                        wait(pe, si_rows, g.n, 2)
                    transposes(bank_l0[j], [cols(adj_in, r, j) for r in range(NB)], adj_t.sem)

            def project_b(g):
                for r in range(NB):
                    wait(pe, alpha_done, g.n, r + 1)
                    product(bank_l0[r], [(cols(a, k, r), b[:, k, :]) for k in range(DB)
                                         for a, b in ((xt_hi, wb_hi), (xt_hi, wb_lo), (xt_lo, wb_hi))],
                            proj_b.sem)

            def hop(g, right_hi, right_lo, signal):
                for r in range(NB):
                    product(bank_l0[r], [(cols(a, j, r), b[:, j, :]) for j in range(NB)
                                         for a, b in ((al_hi, right_hi), (al_hi, right_lo), (al_lo, right_hi))],
                            signal)

            def hop_one(g):
                wait(pe, al_hi_done, g.n, NB)
                wait(pe, al_lo_done, g.n, NB)
                for r in range(NB):
                    wait(pe, y10_done, g.n, r + 1)
                    product(bank_l0[r], [(cols(a, j, r), b[:, j, :]) for j in range(NB)
                                         for a, b in ((al_hi, y2_hi), (al_hi, y2_lo), (al_lo, y2_hi))],
                            hop1.sem)

            def hop_two(g):
                wait(pe, v_hi_done, g.n, 2)
                wait(pe, v_lo_done, g.n, 2)
                for r in range(NB):
                    product(bank_l0[r], [(cols(a, j, r), b[:, j, :]) for j in range(NB)
                                         for a, b in ((al_hi, v_hi), (al_hi, v_lo), (al_lo, v_hi))],
                            hop2.sem)

            def edges_of_x(g):
                wait(pe, inc_done, g.n, 1)
                wait(pe, x1_hi_done, g.n, 1)
                wait(pe, x1_lo_done, g.n, 1)
                for t, e in enumerate(M_ORDER):
                    wait(pe, y_done, g.n - 1, t + 1)
                    product(pc[e], [(cols(inc, c, e), b[:, c, :]) for c in range(NB) for b in (x1_hi, x1_lo)],
                            m_ps.sem)

            def nodes_of_m(g):
                wait(pe, m_hi_done, g.n, NB)
                wait(pe, m_lo_done, g.n, NB)
                wait(pe, inc_t_done, g.n, NB)
                for d in range(DB):
                    product(pc[d], [(cols(a, e, d), inc_t[g.parity][:, e, :])
                                    for e in range(NB) for a in (m_hi, m_lo)], ut_ps.sem)

            def hidden(g):
                wait(pe, ut_hi_done, g.n, DB)
                wait(pe, ut_lo_done, g.n, DB)
                for c in range(NB):
                    product(bank_l1[c], [(cols(a, d, c), b[:, d, :]) for d in range(DB)
                                         for a, b in ((ut_hi, w1t_hi), (ut_hi, w1t_lo), (ut_lo, w1t_hi))],
                            z_ps.sem)

            def transpose_h(g):
                wait(pe, h_done, g.n, NB)
                for k in range(HB):
                    wait(pe, z_done, g.n, k + 1)
                    transposes(bank_l1[k], [cols(h, c, k) for c in range(NB)], ht_ps.sem)

            def hidden_out(g):
                wait(pe, ht_hi_done, g.n, HB)
                wait(pe, ht_lo_done, g.n, HB)
                for c in range(NB):
                    product(bank_l1[c], [(cols(a, k, c), b[:, k, :]) for k in range(HB)
                                         for a, b in ((ht_hi, w2c_hi), (ht_hi, w2c_lo), (ht_lo, w2c_hi))],
                            hw_ps.sem)

            def edges_of_hw(g):
                wait(pe, hw_hi_done, g.n, NB)
                wait(pe, hw_lo_done, g.n, NB)
                for e in range(NB):
                    product(bank_l1[e], [(cols(inc, c, e), b[:, c, :]) for c in range(NB) for b in (hw_hi, hw_lo)],
                            m2_ps.sem)

            def nodes_of_m2(g):
                wait(pe, m2_hi_done, g.n, NB)
                wait(pe, m2_lo_done, g.n, NB)
                for c in range(NB):
                    product(bank_l1[c], [(cols(inc_t[g.parity], e, c), b[:, e, :])
                                         for e in range(NB) for b in (m_hi, m_lo)], y_ps.sem)

            pe.wait_ge(ident_done, 2)
            pe.wait_ge(w1_in, DMA)
            for d in range(DB):
                transposes(pc[d], [cols(w1_f, k, d) for k in range(HB)], set_pe)
            pe.wait_ge(set_dve, SET_BW)
            for b in range(2):
                for t in range(4):
                    k, o = 2 * b + t // 2, t % 2
                    last = nc.tensor.transpose(pc[2 + b][:, t * P:(t + 1) * P], w2_g[:, o, k * P:(k + 1) * P],
                                               ident[:, :])
                last.then_inc(set_pe, 1)
            transposes(pb[2], [bw_rep[:, o, :] for o in range(DB)], set_pe)
            pe.wait_ge(set_dve, SET_END)
            pe.wait_ge(set_act, SET_ACT_END)

            def pair(second, first):
                for step, g in ((transpose_x, first), (edges_of_x, second), (project_a, first),
                                (nodes_of_m, second), (transpose_si, first), (transpose_adj, first),
                                (hidden, second), (project_b, first), (transpose_h, second),
                                (hop_one, first), (hidden_out, second), (hop_two, first),
                                (edges_of_hw, second), (nodes_of_m2, second)):
                    if g is not None:
                        step(g)

            all_graphs(pe, pair)

        @block.scalar
        def _(act):
            def copy(dst, src, signal, scale=1.0):
                nc.scalar.activation(dst, src, ACT.Copy, scale=scale).then_inc(signal, 1)

            def x_hi(g):
                for k in range(DB):
                    wait(act, xt_ps, g.n, k + 1)
                    copy(xt_hi[:, k, :], bank_xt[k][:, :], xt_hi_done.sem)

            def proj_a_hi(g):
                for r in range(NB):
                    wait(act, proj_a, g.n, r + 1)
                    copy(y2_hi[:, r, 0:D], bank_a[r][:, 0:D], y2_hi_done.sem)

            def score_rows(g):
                wait(act, si_ps, g.n, 1)
                wait(act, lrelu_done, g.n - 1, NB)
                copy(si_row[:, :], bank_si[:, :], si_rows.sem)
                copy(si_row2[:, :], bank_si[:, :], si_rows.sem, scale=NEG)

            def exps(g):
                for j in range(NB):
                    wait(act, lrelu_done, g.n, j + 1)
                    nc.scalar.activation(alpha[:, j, :], alpha[:, j, :], ACT.Exp,
                                         bias=score2[:, j:j + 1]).then_inc(exp_done.sem, 1)

            def alpha_hi(g):
                for j in range(NB):
                    wait(act, alpha_done, g.n, j + 1)
                    copy(al_hi[:, j, :], alpha[:, j, :], al_hi_done.sem)

            def proj_b_out(g):
                for r in range(NB):
                    wait(act, proj_b, g.n, r + 1)
                    if r == 0:
                        wait(act, x1_done, g.n - 1, NB)
                    copy(y10[:, r, :], bank_l0[r][:, :], y10_done.sem)

            def v_part_hi(g):
                for s in range(2):
                    wait(act, v_done, g.n, 2 * s + 2)
                    copy(v_hi[:, 2 * s:2 * s + 2, :], y10[:, 2 * s:2 * s + 2, 0:D], v_hi_done.sem)

            def x1_part_hi(g):
                wait(act, x1_done, g.n, NB)
                wait(act, m_ps, g.n - 1, NB)
                copy(x1_hi[:, :, 0:D], x1[:, :, :], x1_hi_done.sem)
                wait(act, y_done, g.n - 2, NB)
                copy(x1_b2[g.parity][:, :, :], x1[:, :, :], x1_twice.sem, scale=2.0)

            def m_part_hi(g):
                for t, e in enumerate(M_ORDER):
                    wait(act, be_done, g.n, 2 * t + 2)
                    copy(m_hi[:, e, :], pc[e][:, 0:D], m_hi_done.sem, scale=be[:, e:e + 1])

            def ut_part_hi(g):
                for d in range(DB):
                    wait(act, ut_ps, g.n, d + 1)
                    copy(ut_hi[:, d, :], pc[d][:, :], ut_hi_done.sem)

            def relu_h(g):
                for c in range(NB):
                    wait(act, z_done, g.n, c + 1)
                    nc.scalar.activation(h[:, c, :], h[:, c, :], ACT.Relu).then_inc(h_done.sem, 1)

            def ht_part_hi(g):
                for k in range(HB):
                    wait(act, ht_ps, g.n, k + 1)
                    copy(ht_hi[:, k, :], bank_l1[k][:, :], ht_hi_done.sem)

            def hw_part_hi(g):
                for c in range(NB):
                    wait(act, hw_done, g.n, c + 1)
                    copy(hw_hi[:, c, :], hw[:, c, :], hw_hi_done.sem)

            def m2_part_hi(g):
                for e in range(NB):
                    wait(act, m2_ps, g.n, e + 1)
                    copy(m_hi[:, e, :], bank_l1[e][:, 0:D], m2_hi_done.sem, scale=be[:, e:e + 1])

            act.wait_ge(set_dve, SET_SCORE)
            act.wait_ge(wk_in, 3 * DMA)
            copy(wa_hi[:, :, :], wa_f, set_act)
            copy(wb_hi[:, :, :], wb_f, set_act)
            for d in range(DB):
                act.wait_ge(set_pe, d + 1)
                copy(w1t_hi[:, d, :], pc[d][:, :], set_act)
            for b in range(2):
                act.wait_ge(set_pe, DB + b + 1)
                copy(w2c_hi[:, 2 * b:2 * b + 2, :], pc[2 + b][:, :].rearrange("p (k c) -> p k c", c=D), set_act)
            act.wait_ge(set_pe, DB + 3)
            copy(bw_row[:, :], pb[2][:, 0:D], set_act)

            def pair(second, first):
                for step, g in ((x_hi, first), (m_part_hi, second), (proj_a_hi, first), (ut_part_hi, second),
                                (score_rows, first), (exps, first), (alpha_hi, first), (relu_h, second),
                                (proj_b_out, first), (ht_part_hi, second), (v_part_hi, first),
                                (hw_part_hi, second), (x1_part_hi, first), (m2_part_hi, second)):
                    if g is not None:
                        step(g)

            all_graphs(act, pair)

        @block.vector
        def _(dve):
            def lo_of(dst, src, hi, signal):
                nc.vector.tensor_tensor(dst, src, f32(hi), ALU.subtract).then_inc(signal, 1)

            def x_lo(g):
                for k in range(DB):
                    wait(dve, xt_hi_done, g.n, k + 1)
                    lo_of(xt_lo[:, k, :], bank_xt[k][:, :], xt_hi[:, k, :], xt_lo_done.sem)

            def proj_a_lo(g):
                for r in range(NB):
                    wait(dve, y2_hi_done, g.n, r + 1)
                    nc.vector.tensor_tensor(scores[:, r, :], bank_a[r][:, D:DA], score_const[:, :],
                                            ALU.add).then_inc(scores_done.sem, 1)
                    lo_of(y2_lo[:, r, :], bank_a[r][:, 0:D], y2_hi[:, r, 0:D], y2_lo_done.sem)
                wait(dve, scores_done, g.n, NB)
                nc.vector.tensor_copy(si_rep[:, :, :], scores[:, :, 1:2].to_broadcast([P, NB, P])
                                      ).then_inc(si_rep_done.sem, 1)
                nc.vector.tensor_scalar(score8[:, :], scores[:, :, 0], 1.0 - NEG, None, ALU.mult
                                        ).then_inc(score_cols.sem, 1)
                nc.vector.tensor_scalar(score2[:, :], scores[:, :, 0], NEG, None, ALU.mult
                                        ).then_inc(score_cols.sem, 1)

            def lrelu(g):
                wait(dve, si_rows, g.n, 2)
                wait(dve, score_cols, g.n, 2)
                for j in range(NB):
                    if j == 0:
                        wait(dve, al_lo_done, g.n - 1, NB)
                    nc.vector.scalar_tensor_tensor(alpha[:, j, :], si_row[:, :], score8[:, j:j + 1],
                                                   si_row2[:, :], ALU.add, ALU.max).then_inc(lrelu_done.sem, 1)

            def incidence_t(g):
                for j in range(NB):
                    wait(dve, adj_t, g.n, j + 1)
                    nc.vector.tensor_scalar(inc_t[g.parity][:, j, :], bank_l0[j][:, :], 0.0, None,
                                            ALU.not_equal).then_inc(inc_t_done.sem, 1)

            def alphas(g):
                for j in range(NB):
                    wait(dve, exp_done, g.n, j + 1)
                    nc.vector.tensor_tensor(alpha[:, j, :], bank_l0[j][:, :], alpha[:, j, :],
                                            ALU.mult).then_inc(alpha_done.sem, 1)

            def first_hop(g):
                for r in range(NB):
                    wait(dve, hop1, g.n, r + 1)
                    nc.vector.tensor_scalar(rowsum[:, r:r + 1], bank_l0[r][:, D:D + 1], 1e-12, None,
                                            ALU.add).then_inc(rowinv_done.sem, 1)
                    wait(dve, rowinv_done, g.n, 2 * r + 1)
                    nc.vector.reciprocal(rowinv[:, r:r + 1], rowsum[:, r:r + 1]).then_inc(rowinv_done.sem, 1)
                    wait(dve, rowinv_done, g.n, 2 * r + 2)
                    nc.vector.scalar_tensor_tensor(y10[:, r, 0:D], bank_l0[r][:, 0:D], rowinv[:, r:r + 1],
                                                   y10[:, r, 0:D], ALU.mult, ALU.add).then_inc(v_done.sem, 1)

            def v_part_lo(g):
                for s in range(2):
                    wait(dve, v_hi_done, g.n, s + 1)
                    lo_of(v_lo[:, 2 * s:2 * s + 2, :], y10[:, 2 * s:2 * s + 2, 0:D],
                          v_hi[:, 2 * s:2 * s + 2, :], v_lo_done.sem)

            def second_hop(g):
                wait(dve, bias_done, g.n, 1)
                for r in range(NB):
                    wait(dve, hop2, g.n, r + 1)
                    nc.vector.scalar_tensor_tensor(y10[:, r, D:2 * D], bank_l0[r][:, 0:D], rowinv[:, r:r + 1],
                                                   y10[:, r, D:2 * D], ALU.mult, ALU.add
                                                   ).then_inc(hop2_read.sem, 1)
                    wait(dve, hop2_read, g.n, r + 1)
                    nc.vector.scalar_tensor_tensor(y10[:, r, D:2 * D], y10[:, r, D:2 * D], 0.0,
                                                   x_in[g.parity][:, r, :], ALU.max, ALU.add
                                                   ).then_inc(res_done.sem, 1)
                    moments(g, y10[:, r, D:2 * D], res_done, stats0, moments0, var0, ln0, r)

            def moments(g, src, made, stats, mean_var, var, ln, r):
                wait(dve, made, g.n, r + 1)
                if r:
                    wait(dve, ln, g.n, max(1, 2 * (r - 1)))
                nc.vector.bn_stats(stats[:, r, :], src).then_inc(ln.sem, 1)
                if r:
                    nc.vector.bn_aggr(mean_var[:, r - 1, :], stats[:, r - 1, :]).then_inc(ln.sem, 1)
                if r == NB - 1:
                    wait(dve, ln, g.n, 2 * NB - 1)
                    nc.vector.tensor_scalar(var[:, 0:r], mean_var[:, 0:r, 1], EPS, None,
                                            ALU.add).then_inc(ln.sem, 1)
                    nc.vector.bn_aggr(mean_var[:, r, :], stats[:, r, :]).then_inc(ln.sem, 1)
                    wait(dve, ln, g.n, 2 * NB + 1)
                    nc.vector.tensor_scalar(var[:, r:r + 1], mean_var[:, r, 1:2], EPS, None,
                                            ALU.add).then_inc(ln.sem, 1)

            def normalise(g, dst, src, mean_var, rstd, done):
                for r in range(NB):
                    nc.vector.tensor_scalar(dst(r), src(r), mean_var[:, r, 0:1], rstd[:, r:r + 1],
                                            ALU.subtract, ALU.mult).then_inc(done.sem, 1)

            def x1_out(g):
                wait(dve, rstd0_done, g.n, 1)
                wait(dve, x1_twice, g.n - 1, 1)
                normalise(g, lambda r: x1[:, r, :], lambda r: y10[:, r, D:2 * D], moments0, rstd0, x1_done)

            def x1_part_lo(g):
                wait(dve, x1_hi_done, g.n, 1)
                lo_of(x1_lo[:, :, :], x1[:, :, :], x1_hi[:, :, 0:D], x1_lo_done.sem)

            def incidence(g):
                wait(dve, m2_ps, g.n - 1, NB)
                wait(dve, adj_loaded, g.n, 1)
                nc.vector.tensor_scalar(inc[:, :, :], adj_in[:, :, :], 0.0, None,
                                        ALU.not_equal).then_inc(inc_done.sem, 1)

            def node_degrees(g):
                wait(dve, w_loaded, g.n, 1)
                total, no_edge, safe, inverse = (deg[:, i, :] for i in range(4))
                for r in range(NB):
                    if r:
                        wait(dve, dn_sum, g.n, r)
                    nc.vector.scalar_tensor_tensor(masked[:, :], adj_in[:, r, :], 0.0, w_row[:, :],
                                                   ALU.not_equal, ALU.mult,
                                                   accum_out=total[:, r:r + 1]).then_inc(dn_sum.sem, 1)
                wait(dve, dn_sum, g.n, NB)
                nc.vector.tensor_scalar(no_edge, total, 0.0, None, ALU.is_le).then_inc(dn_step.sem, 1)
                wait(dve, dn_step, g.n, 1)
                nc.vector.scalar_tensor_tensor(safe, total, 0.0, no_edge, ALU.max, ALU.add
                                               ).then_inc(dn_step.sem, 1)
                wait(dve, dn_step, g.n, 2)
                nc.vector.reciprocal(inverse, safe).then_inc(dn_step.sem, 1)
                wait(dve, dn_step, g.n, 3)
                nc.vector.tensor_tensor(safe, no_edge, inverse, ALU.mult).then_inc(dn_step.sem, 1)
                wait(dve, dn_step, g.n, 4)
                nc.vector.tensor_tensor(dn[g.parity][:, :], inverse, safe, ALU.subtract
                                        ).then_inc(dn_step.sem, 1)

            def m_part_lo(g):
                def inverse(t):
                    e = M_ORDER[t]
                    wait(dve, m_ps, g.n, t + 1)
                    nc.vector.tensor_scalar(be_count[:, e:e + 1], pc[e][:, D:D + 1], 1.0, None,
                                            ALU.max).then_inc(be_done.sem, 1)
                    wait(dve, be_done, g.n, 2 * t + 1)
                    nc.vector.reciprocal(be[:, e:e + 1], be_count[:, e:e + 1]).then_inc(be_done.sem, 1)

                def part(t):
                    e = M_ORDER[t]
                    wait(dve, m_hi_done, g.n, t + 1)
                    nc.vector.scalar_tensor_tensor(m_lo[:, e, :], pc[e][:, 0:D], be[:, e:e + 1],
                                                   f32(m_hi[:, e, :]), ALU.mult, ALU.subtract
                                                   ).then_inc(m_lo_done.sem, 1)

                for t in range(NB):
                    inverse(t)
                    if t:
                        part(t - 1)
                part(NB - 1)

            def ut_part_lo(g):
                for d in range(DB):
                    wait(dve, ut_hi_done, g.n, d + 1)
                    lo_of(ut_lo[:, d, :], pc[d][:, :], ut_hi[:, d, :], ut_lo_done.sem)

            def z_out(g):
                wait(dve, dn_step, g.n, 5)
                for c in range(NB):
                    wait(dve, z_ps, g.n, c + 1)
                    nc.vector.scalar_tensor_tensor(h[:, c, :], bank_l1[c][:, :], dn[g.parity][:, c:c + 1],
                                                   b1_row[:, :], ALU.mult, ALU.add).then_inc(z_done.sem, 1)

            def h_moments(g):
                for c in range(NB):
                    moments(g, h[:, c, :], h_done, stats1, moments1, var1, ln1, c)

            def ht_part_lo(g):
                for k in range(HB):
                    wait(dve, ht_hi_done, g.n, k + 1)
                    lo_of(ht_lo[:, k, :], bank_l1[k][:, :], ht_hi[:, k, :], ht_lo_done.sem)

            def hw_out(g):
                wait(dve, rstd1_done, g.n, 1)
                wait(dve, stored, g.n - 1, 1)
                for c in range(NB):
                    wait(dve, hw_ps, g.n, c + 1)
                    nc.vector.scalar_tensor_tensor(hw[:, c, :], bank_l1[c][:, 0:D], rstd1[:, c:c + 1],
                                                   bw_row[:, :], ALU.mult, ALU.add).then_inc(hw_done.sem, 1)
                    if c:
                        hw_part_lo(g, c - 1)
                hw_part_lo(g, NB - 1)

            def hw_part_lo(g, c):
                wait(dve, hw_hi_done, g.n, c + 1)
                lo_of(hw_lo[:, c, :], hw[:, c, :], hw_hi[:, c, :], hw_lo_done.sem)

            def m2_part_lo(g):
                for e in range(NB):
                    wait(dve, m2_hi_done, g.n, e + 1)
                    nc.vector.scalar_tensor_tensor(m_lo[:, e, :], bank_l1[e][:, 0:D], be[:, e:e + 1],
                                                   f32(m_hi[:, e, :]), ALU.mult, ALU.subtract
                                                   ).then_inc(m2_lo_done.sem, 1)

            def y_out(g):
                wait(dve, x1_b2_done, g.n, 1)
                for c in range(NB):
                    wait(dve, y_ps, g.n, c + 1)
                    nc.vector.scalar_tensor_tensor(y[:, c, :], bank_l1[c][:, 0:D], dn[g.parity][:, c:c + 1],
                                                   x1_b2[g.parity][:, c, :], ALU.mult, ALU.add
                                                   ).then_inc(y_done.sem, 1)
                    if c:
                        y_stats(g, c - 1)
                y_stats(g, NB - 1)

            def y_stats(g, c):
                moments(g, y[:, c, :], y_done, stats2, moments2, var2, ln2, c)

            def result(g):
                wait(dve, rstd2_done, g.n, 1)
                normalise(g, lambda r: y[:, r, :], lambda r: y[:, r, :], moments2, rstd2, out_done)

            steps = [0]

            def then(instruction, wait_for_it=False):
                steps[0] += 1
                instruction.then_inc(set_dve, 1)
                if wait_for_it:
                    dve.wait_ge(set_dve, steps[0])

            def dot(dst, a, b):
                then(nc.vector.scalar_tensor_tensor(masked[:, 0:a.shape[-1]], a, 1.0, b, ALU.mult, ALU.mult,
                                                    accum_out=dst), True)

            then(nc.vector.memset(f32(y2_hi[:, :, D:D + 1]), 1.0))
            then(nc.vector.memset(f32(y2_hi[:, :, D + 1:DA]), 0.0))
            then(nc.vector.memset(f32(x1_hi[:, :, D:D + 1]), 1.0))
            then(nc.vector.memset(f32(x1_hi[:, :, D + 1:DA]), 0.0))
            then(nc.vector.memset(minus_half[:, :], -0.5))
            dve.wait_ge(score_in, 4 * DMA)
            for s in range(2):
                for k in range(DB):
                    dot(wa_f[:, k, D + s:D + s + 1], wv_f[:, k, :], aw_f[:, s * D:(s + 1) * D])
                dot(small[:, s:s + 1], bv_f, aw_f[:, s * D:(s + 1) * D])
            then(nc.vector.tensor_copy(score_const[:, 0:1], small[:, 0:1]))
            then(nc.vector.tensor_tensor(score_const[:, 1:2], small[:, 1:2], ab_f, ALU.add))
            assert steps[0] == SET_SCORE
            dve.wait_ge(w2_in, 3 * DMA)
            for o in range(DB):
                dot(small[:, 2 + o:3 + o], w2_f[:, o, :], beta_f)
            then(nc.vector.tensor_copy(bw_rep, small[:, 2:4].rearrange("p (a b) -> p a b", b=1)
                                       .to_broadcast([P, DB, P])))
            for o in range(DB):
                then(nc.vector.scalar_tensor_tensor(w2_g[:, o, :], w2_f[:, o, :], 1.0, gamma_f, ALU.mult,
                                                    ALU.mult, accum_out=small[:, 4 + o:5 + o]), True)
                then(nc.vector.tensor_scalar(small[:, 6 + o:7 + o], small[:, 4 + o:5 + o], 1.0 / HID, None,
                                             ALU.mult), True)
                then(nc.vector.tensor_scalar(w2_g[:, o, :], w2_g[:, o, :], small[:, 6 + o:7 + o], None,
                                             ALU.subtract), True)
            assert steps[0] == SET_BW
            dve.wait_ge(set_act, 1)
            then(nc.vector.tensor_tensor(wa_lo[:, :, :], wa_f, f32(wa_hi[:, :, :]), ALU.subtract))
            dve.wait_ge(set_act, 2)
            then(nc.vector.tensor_tensor(wb_lo[:, :, :], wb_f, f32(wb_hi[:, :, :]), ALU.subtract))
            for d in range(DB):
                dve.wait_ge(set_act, 3 + d)
                then(nc.vector.tensor_tensor(w1t_lo[:, d, :], pc[d][:, :], f32(w1t_hi[:, d, :]), ALU.subtract))
            for b in range(2):
                dve.wait_ge(set_act, 5 + b)
                then(nc.vector.tensor_tensor(w2c_lo[:, 2 * b:2 * b + 2, :],
                                             pc[2 + b][:, :].rearrange("p (k c) -> p k c", c=D),
                                             f32(w2c_hi[:, 2 * b:2 * b + 2, :]), ALU.subtract))
            dve.wait_ge(rows_in, 3 * DMA)
            then(nc.vector.tensor_tensor(bk_row[:, :], bk_f[:, 0, :], bk_f[:, 1, :], ALU.add), True)
            then(nc.vector.tensor_tensor(bk_row[:, :], bk_row[:, :], bk_f[:, 2, :], ALU.add), True)
            assert steps[0] == SET_END

            def pair(second, first):
                for step, g in ((x_lo, first), (m_part_lo, second), (proj_a_lo, first), (ut_part_lo, second),
                                (lrelu, first), (incidence_t, first), (alphas, first),
                                (z_out, second), (h_moments, second), (ht_part_lo, second),
                                (first_hop, first), (v_part_lo, first), (hw_out, second),
                                (second_hop, first), (incidence, first), (x1_out, first),
                                (x1_part_lo, first), (m2_part_lo, second),
                                (node_degrees, first), (y_out, second), (result, second)):
                    if g is not None:
                        step(g)

            all_graphs(dve, pair)

        @block.gpsimd
        def _(pool):
            def alpha_lo(g):
                for j in range(NB):
                    wait(pool, al_hi_done, g.n, j + 1)
                    if j == 0:
                        wait(pool, hop2, g.n - 1, NB)
                    nc.gpsimd.tensor_tensor(al_lo[:, j, :], alpha[:, j, :], f32(al_hi[:, j, :]),
                                            ALU.subtract).then_inc(al_lo_done.sem, 1)

            def add_bias(g):
                wait(pool, y10_done, g.n, NB)
                nc.gpsimd.tensor_tensor(y10[:, :, D:2 * D], y10[:, :, D:2 * D],
                                        bk_row[:, :].rearrange("p (a c) -> p a c", a=1)
                                        .to_broadcast([P, NB, D]), ALU.add).then_inc(bias_done.sem, 1)

            def inverse_root(g, dst, var, ln, done):
                wait(pool, ln, g.n, LN_STEPS)
                nc.gpsimd.tensor_tensor(dst[:, :], var[:, :], minus_half[:, :], ALU.pow).then_inc(done.sem, 1)

            def root0(g):
                inverse_root(g, rstd0, var0, ln0, rstd0_done)

            def root1(g):
                inverse_root(g, rstd1, var1, ln1, rstd1_done)

            def root2(g):
                inverse_root(g, rstd2, var2, ln2, rstd2_done)

            def add_b2(g):
                wait(pool, x1_twice, g.n, 1)
                nc.gpsimd.tensor_tensor(x1_b2[g.parity][:, :, :], x1_b2[g.parity][:, :, :],
                                        b2_row[:, :].rearrange("p (a c) -> p a c", a=1)
                                        .to_broadcast([P, NB, D]), ALU.add).then_inc(x1_b2_done.sem, 1)

            nc.gpsimd.memset(ident[:, :], 0.0).then_inc(ident_done, 1)
            pool.wait_ge(ident_done, 1)
            nc.gpsimd.affine_select(out=ident[:, :], in_=ident[:, :], compare_op=ALU.not_equal, fill=1.0,
                                    base=0, pattern=[[-1, P]], channel_multiplier=1).then_inc(ident_done, 1)
            pool.wait_ge(set_dve, SET_END)

            def pair(second, first):
                for step, g in ((alpha_lo, first), (root1, second), (add_bias, first), (root0, first),
                                (add_b2, first), (root2, second)):
                    if g is not None:
                        step(g)

            all_graphs(pool, pair)


SET_SCORE = 5 + 6 + 2
SET_BW = SET_SCORE + 2 + 1 + 6
SET_END = SET_BW + 6 + 2
SET_ACT_END = 7


_INS = ["x", "adj", "L0_gnn_Wv", "L0_gnn_bv", "L0_gnn_aw", "L0_gnn_ab", "L0_gnn_Wk", "L0_gnn_bk",
        "L1_gnn_W1", "L1_gnn_b1", "L1_gnn_gamma", "L1_gnn_beta", "L1_gnn_W2", "L1_gnn_b2"]
_OUT = ((16, 512, 256), "float32")


def kernel(**inputs):
    import numpy as _np
    import concourse.bacc as _bacc
    from concourse import mybir as _mybir
    from concourse.bass_utils import run_bass_kernel_spmd as _run

    nc = _bacc.Bacc("TRN2", target_bir_lowering=False, num_devices=1)
    arrays, args = {}, []
    for name in _INS:
        a = _np.ascontiguousarray(inputs[name])
        arrays[f"in_{name}"] = a
        args.append(nc.dram_tensor(f"in_{name}", a.shape, _mybir.dt.from_np(a.dtype), kind="ExternalInput").ap())
    shape, dtype = _OUT
    args.append(nc.dram_tensor("out_0", shape, _mybir.dt.from_np(_np.dtype(dtype)), kind="ExternalOutput").ap())
    gnn_resnorm(nc, *args)
    return _run(nc, [arrays], core_ids=[0]).results[0]["out_0"]
```

```python
from contextlib import ExitStack

import concourse.bass as bass
from concourse import mybir

P = 128
F32 = mybir.dt.float32
F32R = mybir.dt.float32r
ALU = mybir.AluOpType
ACT = mybir.ActivationFunctionType
AX_X = mybir.AxisListType.X
DMA = 16


class Count:

    def __init__(self, sem, per, unit=1):
        self.sem, self.per, self.unit = sem, per, unit

    def value(self, n, k):
        return (n * self.per + k) * self.unit


class Graph:

    def __init__(self, n, parity):
        self.n, self.parity = n, parity


def wait(engine, count, n, k):
    value = count.value(n, k)
    if isinstance(value, int) and value <= 0:
        return
    engine.wait_ge(count.sem, value)


def gnn_resnorm(nc, x, adj, Wv, bv, aw, ab, Wk, bk, W1, b1, gamma, beta, W2, b2, out):
    G, N, D = x.shape
    HID = W1.shape[0]
    NB, DB, HB = N // P, D // P, HID // P
    EPS = 1e-5
    NEG = 0.2
    DA = D + 2
    LN_STEPS = 2 * NB + 2
    assert N == 512 and HID == 512 and D == 256 and G % 2 == 0

    with ExitStack() as ctx:
        def sb(name, shape, dt=F32):
            return ctx.enter_context(nc.sbuf_tensor(name, shape, dt))

        def sem(name):
            return ctx.enter_context(nc.semaphore(name))

        def per_graph(name, per, unit=1):
            return Count(sem(name), per, unit)

        ident = sb("ident", [P, P])
        wa_hi, wa_lo = (sb(f"wa_{s}", [P, DB, DA], F32R) for s in ("hi", "lo"))
        wb_hi, wb_lo = (sb(f"wb_{s}", [P, DB, 2 * D], F32R) for s in ("hi", "lo"))
        w1t_hi, w1t_lo = (sb(f"w1t_{s}", [P, DB, HID], F32R) for s in ("hi", "lo"))
        w2c_hi, w2c_lo = (sb(f"w2c_{s}", [P, HB, D], F32R) for s in ("hi", "lo"))
        score_const = sb("score_const", [P, 2])
        bk_row = sb("bk_row", [P, D])
        b1_row = sb("b1_row", [P, HID])
        b2_row = sb("b2_row", [P, D])
        bw_row = sb("bw_row", [P, D])
        minus_half = sb("minus_half", [P, NB])
        small = sb("small", [P, 16])

        x_in = [sb(f"x_in{i}", [P, NB, D]) for i in range(2)]
        adj_in = sb("adj_in", [P, NB, N])
        w_row = sb("w_row", [P, N])
        xt_hi, xt_lo = (sb(f"xt_{s}", [P, DB, N], F32R) for s in ("hi", "lo"))
        y2_hi = sb("y2_hi", [P, NB, DA], F32R)
        y2_lo = sb("y2_lo", [P, NB, D], F32R)
        y10 = sb("y10", [P, NB, 2 * D])
        scores = sb("scores", [P, NB, 2])
        score8, score2 = sb("score8", [P, NB]), sb("score2", [P, NB])
        si_rep = sb("si_rep", [P, NB, P])
        si_row, si_row2 = sb("si_row", [P, N]), sb("si_row2", [P, N])
        alpha = sb("alpha", [P, NB, N])
        al_hi, al_lo = (sb(f"al_{s}", [P, NB, N], F32R) for s in ("hi", "lo"))
        v_hi, v_lo = (sb(f"v_{s}", [P, NB, D], F32R) for s in ("hi", "lo"))
        rowsum, rowinv = sb("rowsum", [P, NB]), sb("rowinv", [P, NB])
        stats0, moments0 = sb("stats0", [P, NB, 6]), sb("moments0", [P, NB, 2])
        var0, rstd0 = sb("var0", [P, NB]), sb("rstd0", [P, NB])

        x1 = sb("x1", [P, NB, D])
        x1_hi = sb("x1_hi", [P, NB, D], F32R)
        x1_lo = sb("x1_lo", [P, NB, D], F32R)
        x1_b2 = sb("x1_b2", [P, NB, D])
        inc = sb("inc", [P, NB, N], F32R)
        inc_t = [sb(f"inc_t{i}", [P, NB, N], F32R) for i in range(2)]
        deg = sb("deg", [P, 4, NB])
        dn = [sb(f"dn{i}", [P, NB]) for i in range(2)]

        be_count, be_max = sb("be_count", [P, NB]), sb("be_max", [P, NB])
        be = [sb(f"be{i}", [P, NB]) for i in range(2)]
        sign = sb("sign", [P, 2, N])
        m_hi, m_lo = (sb(f"m_{s}", [P, NB, D], F32R) for s in ("hi", "lo"))
        ut_hi, ut_lo = (sb(f"ut_{s}", [P, DB, N], F32R) for s in ("hi", "lo"))
        h = sb("h", [P, NB, HID])
        stats1, moments1 = sb("stats1", [P, NB, 6]), sb("moments1", [P, NB, 2])
        var1, rstd1 = sb("var1", [P, NB]), sb("rstd1", [P, NB])
        ht_hi, ht_lo = (sb(f"ht_{s}", [P, HB, N], F32R) for s in ("hi", "lo"))
        hw = sb("hw", [P, NB, D])
        hw_hi = ut_hi[:, :, :].rearrange("p d (a c) -> p (d a) c", c=D)
        hw_lo = ut_lo[:, :, :].rearrange("p d (a c) -> p (d a) c", c=D)
        y = sb("y", [P, NB, D])
        stats2, moments2 = sb("stats2", [P, NB, 6]), sb("moments2", [P, NB, 2])
        var2, rstd2, shift2 = sb("var2", [P, NB]), sb("rstd2", [P, NB]), sb("shift2", [P, NB])

        pb = [ctx.enter_context(nc.psum_tensor(f"pb{i}", [P, 512], F32)) for i in range(4)]
        pc = [ctx.enter_context(nc.psum_tensor(f"pc{i}", [P, 512], F32)) for i in range(4)]
        bank_xt = [pb[0], pb[1]]
        bank_a = [pb[2], pb[3], pb[0], pb[1]]
        bank_si = pb[2]
        bank_adj = [pb[0], pb[1], pb[3], pb[2]]
        bank_l0 = pb
        M_ORDER = (2, 3, 0, 1)
        bank_l1 = [pc[2], pc[3], pc[0], pc[1]]

        ident_done = sem("ident_done")
        score_in, wk_in, w1_in, w2_in, rows_in = (
            sem(s) for s in ("score_in", "wk_in", "w1_in", "w2_in", "rows_in"))
        set_dve = sem("set_dve")
        set_act = sem("set_act")
        set_pe = sem("set_pe")
        set_pool = sem("set_pool")
        x_loaded, adj_loaded, w_loaded = (
            per_graph(s, 1, DMA) for s in ("x_loaded", "adj_loaded", "w_loaded"))
        stored = per_graph("stored", 1, DMA)
        xt_ps, proj_a, si_ps, adj_t, proj_b, hop1, hop2 = (
            per_graph(s, k) for s, k in (("xt_ps", DB), ("proj_a", NB), ("si_ps", 1), ("adj_t", NB),
                                         ("proj_b", NB), ("hop1", NB), ("hop2", NB)))
        xt_hi_done, xt_lo_done = per_graph("xt_hi_done", DB), per_graph("xt_lo_done", DB)
        y2_hi_done, y2_lo_done = per_graph("y2_hi_done", NB), per_graph("y2_lo_done", NB)
        scores_done, score_cols, si_rep_done = (
            per_graph("scores_done", NB), per_graph("score_cols", 2), per_graph("si_rep_done", 1))
        si_rows = per_graph("si_rows", 2)
        sign_done, inc_t_done = per_graph("sign_done", NB), per_graph("inc_t_done", NB)
        lrelu_done, exp_done, alpha_done = (
            per_graph(s, NB) for s in ("lrelu_done", "exp_done", "alpha_done"))
        al_hi_done, al_lo_done = per_graph("al_hi_done", NB), per_graph("al_lo_done", NB)
        y10_done, bias_done = per_graph("y10_done", NB), per_graph("bias_done", 1)
        rowinv_done = per_graph("rowinv_done", 2 * NB)
        v_done, v_hi_done, v_lo_done = (
            per_graph("v_done", NB), per_graph("v_hi_done", 2), per_graph("v_lo_done", 2))
        hop2_read, res_done, ln0 = per_graph("hop2_read", NB), per_graph("res_done", NB), per_graph("ln0", LN_STEPS)
        rstd0_done = per_graph("rstd0_done", 1)
        x1_done, x1_hi_done, x1_lo_done, x1_b2_done = (
            per_graph(s, k) for s, k in (("x1_done", NB), ("x1_hi_done", 2), ("x1_lo_done", 2),
                                         ("x1_b2_done", 2)))
        inc_done, dn_sum, dn_step = per_graph("inc_done", 1), per_graph("dn_sum", NB), per_graph("dn_step", 5)
        m_ps, ut_ps, z_ps, ht_ps, hw_ps, m2_ps, y_ps = (
            per_graph(s, k) for s, k in (("m_ps", NB), ("ut_ps", DB), ("z_ps", NB), ("ht_ps", HB),
                                         ("hw_ps", NB), ("m2_ps", NB), ("y_ps", NB)))
        be_done = per_graph("be_done", 2)
        m_hi_done, m_lo_done = per_graph("m_hi_done", NB), per_graph("m_lo_done", NB)
        ut_hi_done, ut_lo_done = per_graph("ut_hi_done", DB), per_graph("ut_lo_done", DB)
        z_done, h_done, ln1 = per_graph("z_done", NB), per_graph("h_done", NB), per_graph("ln1", LN_STEPS)
        rstd1_done = per_graph("rstd1_done", 1)
        ht_hi_done, ht_lo_done = per_graph("ht_hi_done", HB), per_graph("ht_lo_done", HB)
        hw_done, hw_hi_done, hw_lo_done = (
            per_graph("hw_done", NB), per_graph("hw_hi_done", NB), per_graph("hw_lo_done", NB))
        m2_hi_done, m2_lo_done = per_graph("m2_hi_done", NB), per_graph("m2_lo_done", NB)
        shift2_done = per_graph("shift2_done", 1)
        y_done, ln2, rstd2_done, out_done = (
            per_graph("y_done", NB), per_graph("ln2", LN_STEPS), per_graph("rstd2_done", 1),
            per_graph("out_done", NB))

        wa_f = alpha[:, 0:2, :].rearrange("p a n -> p (a n)")[:, 0:DB * DA].rearrange(
            "p (k c) -> p k c", c=DA)
        wb_f = alpha[:, 2:4, :]
        w1_f = y10[:, 0:2, :].rearrange("p a (b c) -> p (a b) c", c=D)
        w2_f = y10[:, 2:4, :]
        w2_g = hw[:, :, :].rearrange("p a c -> p (a c)").rearrange("p (o k) -> p o k", k=HID)
        wv_f = h[:, 0, :].rearrange("p (k c) -> p k c", c=D)
        aw_f = h[:, 1, :]
        bv_f = h[:, 2, 0:D]
        ab_f = h[:, 2, D:D + 1]
        gamma_f = h[:, 3, :]
        beta_f = x1[:, 0:2, :].rearrange("p a c -> p (a c)")
        bk_f = x1_b2[:, 0:3, :]
        bw_rep = h[:, 0, 0:DB * P].rearrange("p (o c) -> p o c", c=P)
        left_over = y[:, 0:2, :].rearrange("p a c -> p (a c)")

        def f32(ap):
            return ap.bitcast(F32)

        block = ctx.enter_context(nc.Block())

        def all_graphs(engine, steps):
            def run(*graphs):
                for step, g, *rest in steps(*graphs):
                    if g is not None:
                        step(g, *rest)

            def around(n, parity):
                return [Graph(n + k, (parity + k) % 2) for k in (-1, 0, 1, 2)]

            run(None, None, None, Graph(0, 0))
            run(None, None, Graph(0, 0), Graph(1, 1))
            run(None, *around(0, 0)[1:])
            with engine.Fori(0, (G - 4) // 2) as i:
                run(*around(i * 2 + 1, 1))
                run(*around(i * 2 + 2, 0))
            run(*around(G - 3, 1))
            run(*around(G - 2, 0)[:3], None)
            run(*around(G - 1, 1)[:2], None, None)
            run(Graph(G - 1, 1), None, None, None)

        def once(g):
            return g if g is not None and isinstance(g.n, int) and g.n == 0 else None

        @block.sync
        def _(sp):
            def across(row):
                return row.partition_broadcast(P)

            def load_x(n, parity):
                sp.dma_start(x_in[parity][:, :, :],
                             x[bass.ds(n, 1), :, :].rearrange("g (r p) c -> p (g r) c", p=P)
                             ).then_inc(x_loaded.sem, DMA)

            load_x(0, 0)
            sp.dma_start(wv_f, Wv.rearrange("(k p) c -> p k c", p=P)).then_inc(score_in, DMA)
            sp.dma_start(aw_f, across(aw.rearrange("a b -> (a b)"))).then_inc(score_in, DMA)
            sp.dma_start(bv_f, across(bv)).then_inc(score_in, DMA)
            sp.dma_start(ab_f, across(ab)).then_inc(score_in, DMA)

            def load_adj(n):
                sp.dma_start(adj_in[:, :, :],
                             adj[bass.ds(n, 1), :, :].rearrange("g (r p) c -> p (g r) c", p=P)
                             ).then_inc(adj_loaded.sem, DMA)
                sp.dma_start(w_row[:, :], adj[bass.ds(n, 1), 0:1, :].rearrange("g a c -> (g a c)")
                             .partition_broadcast(P)).then_inc(w_loaded.sem, DMA)

            sp.dma_start(wa_f[:, :, 0:D], Wk[2].rearrange("(k p) c -> p k c", p=P)).then_inc(wk_in, DMA)
            sp.dma_start(wb_f[:, :, 0:D], Wk[1].rearrange("(k p) c -> p k c", p=P)).then_inc(wk_in, DMA)
            sp.dma_start(wb_f[:, :, D:2 * D], Wk[0].rearrange("(k p) c -> p k c", p=P)).then_inc(wk_in, DMA)
            load_adj(0)
            sp.dma_start(w1_f, W1.rearrange("(k p) c -> p k c", p=P)).then_inc(w1_in, DMA)
            sp.dma_start(w2_f, W2.rearrange("(k p) c -> p k c", p=P)).then_inc(w2_in, DMA)
            sp.dma_start(gamma_f, across(gamma)).then_inc(w2_in, DMA)
            sp.dma_start(beta_f, across(beta)).then_inc(w2_in, DMA)
            sp.dma_start(bk_f, across(bk.rearrange("a c -> (a c)")).rearrange("p (a c) -> p a c", c=D)
                         ).then_inc(rows_in, DMA)
            sp.dma_start(b1_row[:, :], across(b1)).then_inc(rows_in, DMA)
            sp.dma_start(b2_row[:, :], across(b2)).then_inc(rows_in, DMA)

            def adj_of(g):
                wait(sp, inc_done, g.n - 1, 1)
                wait(sp, dn_sum, g.n - 1, NB)
                load_adj(g.n)

            def x_after(g):
                wait(sp, x_loaded, g.n, 1)
                wait(sp, res_done, g.n - 1, NB)
                load_x(g.n + 1, 1 - g.parity)

            def pair(first, more=True):
                adj_of(first)
                if more:
                    x_after(first)

            x_after(Graph(0, 0))
            pair(Graph(1, 1))
            with sp.Fori(0, (G - 4) // 2) as i:
                pair(Graph(i * 2 + 2, 0))
                pair(Graph(i * 2 + 3, 1))
            pair(Graph(G - 2, 0))
            pair(Graph(G - 1, 1), more=False)
            wait(sp, stored, G - 1, 1)

        @block.tensor
        def _(pe):
            def product(bank, terms, signal, width=None):
                for t, (left, right) in enumerate(terms):
                    last = nc.tensor.matmul(bank[:, 0:right.shape[-1]], left, right,
                                            start=(t == 0), stop=(t == len(terms) - 1))
                last.then_inc(signal, 1)

            def transposes(bank, blocks, signal):
                for t, block_in in enumerate(blocks):
                    last = nc.tensor.transpose(bank[:, t * P:(t + 1) * P], block_in, ident[:, :])
                last.then_inc(signal, 1)

            def cols(ap, k, b):
                return ap[:, k, b * P:(b + 1) * P]

            def transpose_x(g):
                xs = x_in[g.parity]
                wait(pe, x_loaded, g.n, 1)
                for k in range(DB):
                    wait(pe, hop2_read, g.n - 1, 1 + k)
                    transposes(bank_xt[k], [cols(xs, r, k) for r in range(NB)], xt_ps.sem)

            def project_a(g):
                wait(pe, xt_hi_done, g.n, DB)
                wait(pe, xt_lo_done, g.n, DB)
                if once(g):
                    pe.wait_ge(set_dve, SET_FIRST)
                for r in range(NB):
                    if r < 2:
                        wait(pe, hop2_read, g.n - 1, 3 + r)
                    product(bank_a[r], [(cols(a, k, r), b[:, k, :]) for k in range(DB)
                                        for a, b in ((xt_hi, wa_hi), (xt_hi, wa_lo), (xt_lo, wa_hi))],
                            proj_a.sem)

            def transpose_si(g):
                wait(pe, si_rep_done, g.n, 1)
                wait(pe, y2_lo_done, g.n, 1)
                transposes(bank_si, [si_rep[:, r, :] for r in range(NB)], si_ps.sem)

            def transpose_adj(g, *blocks):
                wait(pe, adj_loaded, g.n, 1)
                for j in blocks:
                    if j < NB - 1:
                        wait(pe, y2_lo_done, g.n, bank_a.index(bank_adj[j]) + 1)
                        wait(pe, scores_done, g.n, bank_a.index(bank_adj[j]) + 1)
                    else:
                        wait(pe, si_rows, g.n, 2)
                    transposes(bank_adj[j], [cols(adj_in, r, j) for r in range(NB)], adj_t.sem)

            def project_b(g):
                for r in range(NB):
                    wait(pe, alpha_done, g.n, bank_adj.index(bank_l0[r]) + 1)
                    product(bank_l0[r], [(cols(a, k, r), b[:, k, :]) for k in range(DB)
                                         for a, b in ((xt_hi, wb_hi), (xt_hi, wb_lo), (xt_lo, wb_hi))],
                            proj_b.sem)

            def hop_one(g):
                wait(pe, al_hi_done, g.n, NB)
                wait(pe, al_lo_done, g.n, NB)
                for r in range(NB):
                    wait(pe, y10_done, g.n, r + 1)
                    product(bank_l0[r], [(cols(a, j, r), b[:, j, :]) for j in range(NB)
                                         for a, b in ((al_hi, y2_hi), (al_hi, y2_lo), (al_lo, y2_hi))],
                            hop1.sem)

            def hop_two(g):
                wait(pe, v_hi_done, g.n, 2)
                wait(pe, v_lo_done, g.n, 2)
                for r in range(NB):
                    product(bank_l0[r], [(cols(a, j, r), b[:, j, :]) for j in range(NB)
                                         for a, b in ((al_hi, v_hi), (al_hi, v_lo), (al_lo, v_hi))],
                            hop2.sem)

            def edges_of_x(g):
                wait(pe, inc_done, g.n, 1)
                wait(pe, x1_hi_done, g.n, 2)
                wait(pe, x1_lo_done, g.n, 2)
                for t, e in enumerate(M_ORDER):
                    wait(pe, y_done, g.n - 1, t + 1)
                    product(pc[e], [(cols(inc, c, e), b[:, c, :]) for c in range(NB) for b in (x1_hi, x1_lo)],
                            m_ps.sem)

            def nodes_of_m(g):
                wait(pe, m_hi_done, g.n, NB)
                wait(pe, m_lo_done, g.n, NB)
                wait(pe, inc_t_done, g.n, NB)
                for d in range(DB):
                    product(pc[d], [(cols(a, e, d), inc_t[g.parity][:, e, :])
                                    for e in range(NB) for a in (m_hi, m_lo)], ut_ps.sem)

            def hidden(g):
                wait(pe, ut_hi_done, g.n, DB)
                wait(pe, ut_lo_done, g.n, DB)
                if once(g):
                    pe.wait_ge(set_dve, SET_END)
                for c in range(NB):
                    product(bank_l1[c], [(cols(a, d, c), b[:, d, :]) for d in range(DB)
                                         for a, b in ((ut_hi, w1t_hi), (ut_hi, w1t_lo), (ut_lo, w1t_hi))],
                            z_ps.sem)

            def transpose_h(g):
                wait(pe, h_done, g.n, NB)
                for k in range(HB):
                    wait(pe, z_done, g.n, k + 1)
                    transposes(bank_l1[k], [cols(h, c, k) for c in range(NB)], ht_ps.sem)

            def hidden_out(g):
                wait(pe, ht_hi_done, g.n, HB)
                wait(pe, ht_lo_done, g.n, HB)
                for c in range(NB):
                    product(bank_l1[c], [(cols(a, k, c), b[:, k, :]) for k in range(HB)
                                         for a, b in ((ht_hi, w2c_hi), (ht_hi, w2c_lo), (ht_lo, w2c_hi))],
                            hw_ps.sem)

            def edges_of_hw(g):
                wait(pe, hw_hi_done, g.n, NB)
                wait(pe, hw_lo_done, g.n, NB)
                for e in range(NB):
                    product(bank_l1[e], [(cols(inc, c, e), b[:, c, :]) for c in range(NB) for b in (hw_hi, hw_lo)],
                            m2_ps.sem)

            def nodes_of_m2(g):
                wait(pe, m2_hi_done, g.n, NB)
                wait(pe, m2_lo_done, g.n, NB)
                for c in range(NB):
                    product(bank_l1[c], [(cols(inc_t[g.parity], e, c), b[:, e, :])
                                         for e in range(NB) for b in (m_hi, m_lo)], y_ps.sem)

            def second_weights(g):
                pe.wait_ge(w1_in, DMA)
                for d in range(DB):
                    transposes(pc[d], [cols(w1_f, k, d) for k in range(HB)], set_pe)
                pe.wait_ge(set_dve, SET_BW)
                for b in range(2):
                    transposes(pc[2 + b], [w2_g[:, o, k * P:(k + 1) * P] for k in (2 * b, 2 * b + 1)
                                           for o in range(DB)], set_pe)
                pe.wait_ge(set_dve, SET_BW + 1)
                transposes(pc[0], [bw_rep[:, o, :] for o in range(DB)], set_pe)

            pe.wait_ge(ident_done, 2)

            def steps(done, second, first, after):
                return ((edges_of_x, second), (transpose_si, first), (transpose_adj, first, 0, 1),
                        (nodes_of_m, second), (transpose_adj, first, 2, 3), (second_weights, once(first)),
                        (hidden, second), (project_b, first), (transpose_h, second), (hop_one, first),
                        (hidden_out, second), (hop_two, first), (transpose_x, after),
                        (edges_of_hw, second), (project_a, after), (nodes_of_m2, second))

            all_graphs(pe, steps)

        @block.scalar
        def _(act):
            def copy(dst, src, signal, scale=1.0):
                nc.scalar.activation(dst, src, ACT.Copy, scale=scale).then_inc(signal, 1)

            def x_hi(g):
                for k in range(DB):
                    wait(act, xt_ps, g.n, k + 1)
                    copy(xt_hi[:, k, :], bank_xt[k][:, :], xt_hi_done.sem)

            def proj_a_hi(g):
                for r in range(NB):
                    wait(act, proj_a, g.n, r + 1)
                    copy(y2_hi[:, r, 0:D], bank_a[r][:, 0:D], y2_hi_done.sem)

            def score_rows(g):
                wait(act, si_ps, g.n, 1)
                wait(act, lrelu_done, g.n - 1, NB)
                copy(si_row[:, :], bank_si[:, :], si_rows.sem)
                copy(si_row2[:, :], bank_si[:, :], si_rows.sem, scale=NEG)

            def exps(g, *blocks):
                for j in blocks:
                    wait(act, lrelu_done, g.n, j + 1)
                    nc.scalar.activation(alpha[:, j, :], alpha[:, j, :], ACT.Exp,
                                         bias=score2[:, j:j + 1]).then_inc(exp_done.sem, 1)

            def incidence_t(g, *blocks):
                for j in blocks:
                    wait(act, adj_t, g.n, j + 1)
                    wait(act, inc_t_done, g.n, j - 1)
                    nc.scalar.activation(sign[:, j % 2, :], bank_adj[j][:, :], ACT.Sign
                                         ).then_inc(sign_done.sem, 1)
                    wait(act, sign_done, g.n, j + 1)
                    if j == 0:
                        wait(act, be_done, g.n - 1, 1)
                    nc.scalar.activation(inc_t[g.parity][:, j, :], sign[:, j % 2, :], ACT.Square,
                                         accum_out=be_count[:, j:j + 1]).then_inc(inc_t_done.sem, 1)

            def alpha_hi(g):
                for j in range(NB):
                    wait(act, alpha_done, g.n, j + 1)
                    copy(al_hi[:, j, :], alpha[:, j, :], al_hi_done.sem)

            def proj_b_out(g):
                for r in range(NB):
                    wait(act, proj_b, g.n, r + 1)
                    if r == 0:
                        wait(act, x1_done, g.n - 1, NB)
                    copy(y10[:, r, :], bank_l0[r][:, :], y10_done.sem)

            def v_part_hi(g):
                for s in range(2):
                    wait(act, v_done, g.n, 2 * s + 2)
                    copy(v_hi[:, 2 * s:2 * s + 2, :], y10[:, 2 * s:2 * s + 2, 0:D], v_hi_done.sem)

            def x1_part_hi(g, s):
                wait(act, m_ps, g.n - 1, NB)
                wait(act, x1_done, g.n, 2 * s + 2)
                copy(x1_hi[:, 2 * s:2 * s + 2, :], x1[:, 2 * s:2 * s + 2, :], x1_hi_done.sem)

            def m_part_hi(g):
                for t, e in enumerate(M_ORDER):
                    wait(act, m_ps, g.n, t + 1)
                    wait(act, be_done, g.n, 2)
                    copy(m_hi[:, e, :], pc[e][:, 0:D], m_hi_done.sem, scale=be[g.parity][:, e:e + 1])

            def ut_part_hi(g, d):
                wait(act, ut_ps, g.n, d + 1)
                copy(ut_hi[:, d, :], pc[d][:, :], ut_hi_done.sem)

            def result(g):
                wait(act, shift2_done, g.n, 1)
                for c in range(NB):
                    nc.scalar.activation(y[:, c, :], y[:, c, :], ACT.Identity, bias=shift2[:, c:c + 1],
                                         scale=rstd2[:, c:c + 1]).then_inc(out_done.sem, 1)

            def relu_h(g):
                for c in range(NB):
                    wait(act, z_done, g.n, c + 1)
                    nc.scalar.activation(h[:, c, :], h[:, c, :], ACT.Relu).then_inc(h_done.sem, 1)

            def ht_part_hi(g):
                for k in range(HB):
                    wait(act, ht_ps, g.n, k + 1)
                    copy(ht_hi[:, k, :], bank_l1[k][:, :], ht_hi_done.sem)

            def hw_part_hi(g):
                for c in range(NB):
                    wait(act, hw_done, g.n, c + 1)
                    copy(hw_hi[:, c, :], hw[:, c, :], hw_hi_done.sem)

            def m2_part_hi(g):
                for e in range(NB):
                    wait(act, m2_ps, g.n, e + 1)
                    copy(m_hi[:, e, :], bank_l1[e][:, 0:D], m2_hi_done.sem, scale=be[g.parity][:, e:e + 1])

            def second_weights(g):
                for d in range(DB):
                    act.wait_ge(set_pe, d + 1)
                    copy(w1t_hi[:, d, :], pc[d][:, :], set_act)
                for b in range(2):
                    act.wait_ge(set_pe, DB + b + 1)
                    copy(w2c_hi[:, 2 * b:2 * b + 2, :], pc[2 + b][:, :].rearrange("p (k c) -> p k c", c=D),
                         set_act)
                act.wait_ge(set_pe, DB + 3)
                copy(bw_row[:, :], pc[0][:, 0:D], set_act)

            act.wait_ge(wk_in, 3 * DMA)
            copy(wb_hi[:, :, :], wb_f, set_act)
            act.wait_ge(set_dve, SET_SCORE)
            copy(wa_hi[:, :, :], wa_f, set_act)

            def steps(done, second, first, after):
                return ((m_part_hi, second), (score_rows, first), (incidence_t, first, 0),
                        (ut_part_hi, second, 0), (exps, first, 0), (ut_part_hi, second, 1),
                        (incidence_t, first, 1), (exps, first, 1, 2, 3), (incidence_t, first, 2, 3),
                        (second_weights, once(first)), (alpha_hi, first), (relu_h, second), (proj_b_out, first),
                        (ht_part_hi, second), (result, done), (v_part_hi, first), (hw_part_hi, second),
                        (x_hi, after), (m2_part_hi, second), (x1_part_hi, first, 0),
                        (x1_part_hi, first, 1), (proj_a_hi, after))

            all_graphs(act, steps)

        @block.vector
        def _(dve):
            def lo_of(dst, src, hi, signal):
                nc.vector.tensor_tensor(dst, src, f32(hi), ALU.subtract).then_inc(signal, 1)

            def x_lo(g, k):
                wait(dve, xt_hi_done, g.n, k + 1)
                lo_of(xt_lo[:, k, :], bank_xt[k][:, :], xt_hi[:, k, :], xt_lo_done.sem)

            def proj_a_lo(g):
                for r in range(NB):
                    wait(dve, y2_hi_done, g.n, r + 1)
                    nc.vector.tensor_tensor(scores[:, r, :], bank_a[r][:, D:DA], score_const[:, :],
                                            ALU.add).then_inc(scores_done.sem, 1)
                    lo_of(y2_lo[:, r, :], bank_a[r][:, 0:D], y2_hi[:, r, 0:D], y2_lo_done.sem)
                wait(dve, scores_done, g.n, NB)
                nc.vector.tensor_copy(si_rep[:, :, :], scores[:, :, 1:2].to_broadcast([P, NB, P])
                                      ).then_inc(si_rep_done.sem, 1)
                nc.vector.tensor_scalar(score8[:, :], scores[:, :, 0], 1.0 - NEG, None, ALU.mult
                                        ).then_inc(score_cols.sem, 1)
                nc.vector.tensor_scalar(score2[:, :], scores[:, :, 0], NEG, None, ALU.mult
                                        ).then_inc(score_cols.sem, 1)

            def lrelu(g, *blocks):
                wait(dve, si_rows, g.n, 2)
                wait(dve, score_cols, g.n, 2)
                for j in blocks:
                    if j == 0:
                        wait(dve, dn_sum, g.n - 1, NB)
                    nc.vector.scalar_tensor_tensor(alpha[:, j, :], si_row[:, :], score8[:, j:j + 1],
                                                   si_row2[:, :], ALU.add, ALU.max).then_inc(lrelu_done.sem, 1)

            def alphas(g):
                for j in range(NB):
                    wait(dve, exp_done, g.n, j + 1)
                    wait(dve, sign_done, g.n, j + 1)
                    nc.vector.tensor_tensor(alpha[:, j, :], bank_adj[j][:, :], alpha[:, j, :],
                                            ALU.mult).then_inc(alpha_done.sem, 1)

            def first_hop(g):
                for r in range(NB):
                    wait(dve, hop1, g.n, r + 1)
                    nc.vector.tensor_scalar(rowsum[:, r:r + 1], bank_l0[r][:, D:D + 1], 1e-12, None,
                                            ALU.add).then_inc(rowinv_done.sem, 1)
                    wait(dve, rowinv_done, g.n, 2 * r + 1)
                    nc.vector.reciprocal(rowinv[:, r:r + 1], rowsum[:, r:r + 1]).then_inc(rowinv_done.sem, 1)
                    wait(dve, rowinv_done, g.n, 2 * r + 2)
                    nc.vector.scalar_tensor_tensor(y10[:, r, 0:D], bank_l0[r][:, 0:D], rowinv[:, r:r + 1],
                                                   y10[:, r, 0:D], ALU.mult, ALU.add).then_inc(v_done.sem, 1)

            def second_hop(g, *rows):
                wait(dve, bias_done, g.n, 1)
                for r in rows:
                    wait(dve, hop2, g.n, r + 1)
                    nc.vector.scalar_tensor_tensor(y10[:, r, D:2 * D], bank_l0[r][:, 0:D], rowinv[:, r:r + 1],
                                                   y10[:, r, D:2 * D], ALU.mult, ALU.add
                                                   ).then_inc(hop2_read.sem, 1)
                    wait(dve, hop2_read, g.n, r + 1)
                    nc.vector.scalar_tensor_tensor(y10[:, r, D:2 * D], y10[:, r, D:2 * D], 0.0,
                                                   x_in[g.parity][:, r, :], ALU.max, ALU.add
                                                   ).then_inc(res_done.sem, 1)
                    moments(g, y10[:, r, D:2 * D], res_done, stats0, moments0, var0, ln0, r)

            def moments(g, src, made, stats, mean_var, var, ln, r):
                wait(dve, made, g.n, r + 1)
                if r:
                    wait(dve, ln, g.n, max(1, 2 * (r - 1)))
                nc.vector.bn_stats(stats[:, r, :], src).then_inc(ln.sem, 1)
                if r:
                    nc.vector.bn_aggr(mean_var[:, r - 1, :], stats[:, r - 1, :]).then_inc(ln.sem, 1)
                if r == NB - 1:
                    wait(dve, ln, g.n, 2 * NB - 1)
                    nc.vector.tensor_scalar(var[:, 0:r], mean_var[:, 0:r, 1], EPS, None,
                                            ALU.add).then_inc(ln.sem, 1)
                    nc.vector.bn_aggr(mean_var[:, r, :], stats[:, r, :]).then_inc(ln.sem, 1)
                    wait(dve, ln, g.n, 2 * NB + 1)
                    nc.vector.tensor_scalar(var[:, r:r + 1], mean_var[:, r, 1:2], EPS, None,
                                            ALU.add).then_inc(ln.sem, 1)

            def normalise(g, dst, src, mean_var, rstd, done):
                for r in range(NB):
                    nc.vector.tensor_scalar(dst(r), src(r), mean_var[:, r, 0:1], rstd[:, r:r + 1],
                                            ALU.subtract, ALU.mult).then_inc(done.sem, 1)

            def x1_out(g):
                wait(dve, rstd0_done, g.n, 1)
                wait(dve, x1_b2_done, g.n - 1, 2)
                normalise(g, lambda r: x1[:, r, :], lambda r: y10[:, r, D:2 * D], moments0, rstd0, x1_done)

            def incidence(g):
                wait(dve, m2_ps, g.n - 1, NB)
                wait(dve, adj_loaded, g.n, 1)
                nc.vector.tensor_scalar(inc[:, :, :], adj_in[:, :, :], 0.0, None,
                                        ALU.not_equal).then_inc(inc_done.sem, 1)

            def degree_sums(g, r):
                wait(dve, adj_loaded, g.n, 1)
                wait(dve, w_loaded, g.n, 1)
                wait(dve, al_lo_done, g.n, NB)
                nc.vector.scalar_tensor_tensor(alpha[:, r, :], adj_in[:, r, :], 0.0, w_row[:, :],
                                               ALU.not_equal, ALU.mult,
                                               accum_out=deg[:, 0, r:r + 1]).then_inc(dn_sum.sem, 1)

            def degree_inverses(g):
                total, no_edge, safe, inverse = (deg[:, i, :] for i in range(4))
                wait(dve, dn_sum, g.n, NB)
                nc.vector.tensor_scalar(no_edge, total, 0.0, None, ALU.is_le).then_inc(dn_step.sem, 1)
                wait(dve, dn_step, g.n, 1)
                nc.vector.scalar_tensor_tensor(safe, total, 0.0, no_edge, ALU.max, ALU.add
                                               ).then_inc(dn_step.sem, 1)
                wait(dve, dn_step, g.n, 2)
                nc.vector.reciprocal(inverse, safe).then_inc(dn_step.sem, 1)
                wait(dve, dn_step, g.n, 3)
                nc.vector.tensor_tensor(safe, no_edge, inverse, ALU.mult).then_inc(dn_step.sem, 1)
                wait(dve, dn_step, g.n, 4)
                nc.vector.tensor_tensor(dn[g.parity][:, :], inverse, safe, ALU.subtract
                                        ).then_inc(dn_step.sem, 1)

            def edge_inverses(g):
                wait(dve, inc_t_done, g.n, NB)
                nc.vector.tensor_scalar(be_max[:, :], be_count[:, :], 1.0, None, ALU.max
                                        ).then_inc(be_done.sem, 1)
                wait(dve, be_done, g.n, 1)
                nc.vector.reciprocal(be[g.parity][:, :], be_max[:, :]).then_inc(be_done.sem, 1)

            def m_part_lo(g):
                for t, e in enumerate(M_ORDER):
                    wait(dve, m_hi_done, g.n, t + 1)
                    nc.vector.scalar_tensor_tensor(m_lo[:, e, :], pc[e][:, 0:D], be[g.parity][:, e:e + 1],
                                                   f32(m_hi[:, e, :]), ALU.mult, ALU.subtract
                                                   ).then_inc(m_lo_done.sem, 1)

            def ut_part_lo(g, d):
                wait(dve, ut_hi_done, g.n, d + 1)
                lo_of(ut_lo[:, d, :], pc[d][:, :], ut_hi[:, d, :], ut_lo_done.sem)

            def z_out(g):
                wait(dve, dn_step, g.n, 5)
                for c in range(NB):
                    wait(dve, z_ps, g.n, c + 1)
                    nc.vector.scalar_tensor_tensor(h[:, c, :], bank_l1[c][:, :], dn[g.parity][:, c:c + 1],
                                                   b1_row[:, :], ALU.mult, ALU.add).then_inc(z_done.sem, 1)

            def h_moments(g):
                for c in range(NB):
                    moments(g, h[:, c, :], h_done, stats1, moments1, var1, ln1, c)

            def ht_part_lo(g):
                for k in range(HB):
                    wait(dve, ht_hi_done, g.n, k + 1)
                    lo_of(ht_lo[:, k, :], bank_l1[k][:, :], ht_hi[:, k, :], ht_lo_done.sem)

            def hw_out(g, c):
                wait(dve, rstd1_done, g.n, 1)
                wait(dve, hw_ps, g.n, c + 1)
                nc.vector.scalar_tensor_tensor(hw[:, c, :], bank_l1[c][:, 0:D], rstd1[:, c:c + 1],
                                               bw_row[:, :], ALU.mult, ALU.add).then_inc(hw_done.sem, 1)

            def m2_part_lo(g):
                for e in range(NB):
                    wait(dve, m2_hi_done, g.n, e + 1)
                    nc.vector.scalar_tensor_tensor(m_lo[:, e, :], bank_l1[e][:, 0:D], be[g.parity][:, e:e + 1],
                                                   f32(m_hi[:, e, :]), ALU.mult, ALU.subtract
                                                   ).then_inc(m2_lo_done.sem, 1)

            def y_out(g, c):
                if c == 0:
                    wait(dve, x1_b2_done, g.n, 2)
                    wait(dve, stored, g.n - 1, 1)
                wait(dve, y_ps, g.n, c + 1)
                nc.vector.scalar_tensor_tensor(y[:, c, :], bank_l1[c][:, 0:D], dn[g.parity][:, c:c + 1],
                                               x1_b2[:, c, :], ALU.mult, ALU.add
                                               ).then_inc(y_done.sem, 1)

            def y_moments(g):
                for c in range(NB):
                    moments(g, y[:, c, :], y_done, stats2, moments2, var2, ln2, c)

            def result_shift(g):
                wait(dve, rstd2_done, g.n, 1)
                wait(dve, out_done, g.n - 1, NB)
                nc.vector.scalar_tensor_tensor(shift2[:, :], moments2[:, :, 0], -1.0, rstd2[:, :],
                                               ALU.mult, ALU.mult).then_inc(shift2_done.sem, 1)

            steps_done = [0]

            def then(instruction, wait_for_it=False):
                steps_done[0] += 1
                instruction.then_inc(set_dve, 1)
                if wait_for_it:
                    dve.wait_ge(set_dve, steps_done[0])

            def dot(dst, a, b):
                then(nc.vector.scalar_tensor_tensor(left_over[:, 0:a.shape[-1]], a, 1.0, b, ALU.mult, ALU.mult,
                                                    accum_out=dst), True)

            then(nc.vector.memset(f32(y2_hi[:, :, D:D + 1]), 1.0))
            then(nc.vector.memset(f32(y2_hi[:, :, D + 1:DA]), 0.0))
            then(nc.vector.memset(minus_half[:, :], -0.5))
            dve.wait_ge(score_in, 4 * DMA)
            for s in range(2):
                for k in range(DB):
                    dot(wa_f[:, k, D + s:D + s + 1], wv_f[:, k, :], aw_f[:, s * D:(s + 1) * D])
                dot(small[:, s:s + 1], bv_f, aw_f[:, s * D:(s + 1) * D])
            then(nc.vector.tensor_copy(score_const[:, 0:1], small[:, 0:1]))
            then(nc.vector.tensor_tensor(score_const[:, 1:2], small[:, 1:2], ab_f, ALU.add))
            assert steps_done[0] == SET_SCORE
            dve.wait_ge(set_act, 1)
            then(nc.vector.tensor_tensor(wb_lo[:, :, :], wb_f, f32(wb_hi[:, :, :]), ALU.subtract))
            dve.wait_ge(set_act, 2)
            then(nc.vector.tensor_tensor(wa_lo[:, :, :], wa_f, f32(wa_hi[:, :, :]), ALU.subtract))
            assert steps_done[0] == SET_FIRST

            def second_weights(g):
                dve.wait_ge(w2_in, 3 * DMA)
                for o in range(DB):
                    then(nc.vector.scalar_tensor_tensor(w2_g[:, o, :], w2_f[:, o, :], 1.0, gamma_f, ALU.mult,
                                                        ALU.mult, accum_out=small[:, 4 + o:5 + o]), True)
                    then(nc.vector.tensor_scalar(small[:, 6 + o:7 + o], small[:, 4 + o:5 + o], 1.0 / HID,
                                                 None, ALU.mult), True)
                    then(nc.vector.tensor_scalar(w2_g[:, o, :], w2_g[:, o, :], small[:, 6 + o:7 + o], None,
                                                 ALU.subtract), True)
                for o in range(DB):
                    dot(small[:, 2 + o:3 + o], w2_f[:, o, :], beta_f)
                then(nc.vector.tensor_copy(bw_rep, small[:, 2:4].rearrange("p (a b) -> p a b", b=1)
                                           .to_broadcast([P, DB, P])))
                assert steps_done[0] == SET_BW
                for d in range(DB):
                    dve.wait_ge(set_act, 3 + d)
                    then(nc.vector.tensor_tensor(w1t_lo[:, d, :], pc[d][:, :], f32(w1t_hi[:, d, :]),
                                                 ALU.subtract))
                for b in range(2):
                    dve.wait_ge(set_act, 5 + b)
                    then(nc.vector.tensor_tensor(w2c_lo[:, 2 * b:2 * b + 2, :],
                                                 pc[2 + b][:, :].rearrange("p (k c) -> p k c", c=D),
                                                 f32(w2c_hi[:, 2 * b:2 * b + 2, :]), ALU.subtract))
                dve.wait_ge(rows_in, 3 * DMA)
                then(nc.vector.tensor_tensor(bk_row[:, :], bk_f[:, 0, :], bk_f[:, 1, :], ALU.add), True)
                then(nc.vector.tensor_tensor(bk_row[:, :], bk_row[:, :], bk_f[:, 2, :], ALU.add), True)
                dve.wait_ge(set_act, SET_ACT_END)
                assert steps_done[0] == SET_END

            def steps(done, second, first, after):
                return ((m_part_lo, second), (lrelu, first, 0, 1, 2),
                        (ut_part_lo, second, 0), (lrelu, first, 3), (ut_part_lo, second, 1), (y_moments, done),
                        (edge_inverses, first), (alphas, first), (second_weights, once(first)),
                        (z_out, second), (h_moments, second), (result_shift, done),
                        (ht_part_lo, second), (first_hop, first),
                        (hw_out, second, 0), (degree_sums, first, 0), (hw_out, second, 1),
                        (degree_sums, first, 1), (hw_out, second, 2), (degree_sums, first, 2),
                        (hw_out, second, 3), (degree_sums, first, 3), (degree_inverses, first),
                        (second_hop, first, 0, 1, 2), (x_lo, after, 0), (x_lo, after, 1),
                        (second_hop, first, 3), (m2_part_lo, second), (x1_out, first),
                        (incidence, first), (y_out, second, 0), (y_out, second, 1),
                        (proj_a_lo, after), (y_out, second, 2), (y_out, second, 3))

            all_graphs(dve, steps)

        @block.gpsimd
        def _(pool):
            def alpha_lo(g):
                for j in range(NB):
                    wait(pool, al_hi_done, g.n, j + 1)
                    if j == 0:
                        wait(pool, hop2, g.n - 1, NB)
                    nc.gpsimd.tensor_tensor(al_lo[:, j, :], alpha[:, j, :], f32(al_hi[:, j, :]),
                                            ALU.subtract).then_inc(al_lo_done.sem, 1)

            def v_part_lo(g):
                for s in range(2):
                    wait(pool, v_hi_done, g.n, s + 1)
                    nc.gpsimd.tensor_tensor(v_lo[:, 2 * s:2 * s + 2, :], y10[:, 2 * s:2 * s + 2, 0:D],
                                            f32(v_hi[:, 2 * s:2 * s + 2, :]), ALU.subtract
                                            ).then_inc(v_lo_done.sem, 1)

            def hw_part_lo(g):
                for c in range(NB):
                    wait(pool, hw_hi_done, g.n, c + 1)
                    nc.gpsimd.tensor_tensor(hw_lo[:, c, :], hw[:, c, :], f32(hw_hi[:, c, :]), ALU.subtract
                                            ).then_inc(hw_lo_done.sem, 1)

            def add_bias(g):
                wait(pool, y10_done, g.n, NB)
                if once(g):
                    pool.wait_ge(set_dve, SET_END)
                nc.gpsimd.tensor_tensor(y10[:, :, D:2 * D], y10[:, :, D:2 * D],
                                        bk_row[:, :].rearrange("p (a c) -> p a c", a=1)
                                        .to_broadcast([P, NB, D]), ALU.add).then_inc(bias_done.sem, 1)

            def inverse_root(g, dst, var, ln, done):
                wait(pool, ln, g.n, LN_STEPS)
                nc.gpsimd.tensor_tensor(dst[:, :], var[:, :], minus_half[:, :], ALU.pow).then_inc(done.sem, 1)

            def root0(g):
                inverse_root(g, rstd0, var0, ln0, rstd0_done)

            def root1(g):
                inverse_root(g, rstd1, var1, ln1, rstd1_done)

            def root2(g):
                inverse_root(g, rstd2, var2, ln2, rstd2_done)

            def x1_part_lo(g):
                for s in range(2):
                    wait(pool, x1_hi_done, g.n, s + 1)
                    nc.gpsimd.tensor_tensor(x1_lo[:, 2 * s:2 * s + 2, :], x1[:, 2 * s:2 * s + 2, :],
                                            f32(x1_hi[:, 2 * s:2 * s + 2, :]), ALU.subtract
                                            ).then_inc(x1_lo_done.sem, 1)

            def double_x1(g):
                wait(pool, y_done, g.n - 1, NB)
                wait(pool, x1_done, g.n, NB)
                nc.gpsimd.tensor_tensor(x1_b2[:, :, :], x1[:, :, :], b2_row[:, :].rearrange(
                    "p (a c) -> p a c", a=1).to_broadcast([P, NB, D]), ALU.add).then_inc(x1_b2_done.sem, 1)
                wait(pool, x1_b2_done, g.n, 1)
                nc.gpsimd.tensor_tensor(x1_b2[:, :, :], x1_b2[:, :, :], x1[:, :, :], ALU.add
                                        ).then_inc(x1_b2_done.sem, 1)

            def store(g):
                wait(pool, out_done, g.n, NB)
                pool.dma_start(out[bass.ds(g.n, 1), :, :].rearrange("g (r p) c -> p (g r) c", p=P),
                             y[:, :, :]).then_inc(stored.sem, DMA)

            nc.gpsimd.memset(ident[:, :], 0.0).then_inc(ident_done, 1)
            pool.wait_ge(ident_done, 1)
            nc.gpsimd.affine_select(out=ident[:, :], in_=ident[:, :], compare_op=ALU.not_equal, fill=1.0,
                                    base=0, pattern=[[-1, P]], channel_multiplier=1).then_inc(ident_done, 1)

            def steps(done, second, first, after):
                return ((root2, done), (alpha_lo, first), (root1, second), (add_bias, first),
                        (store, done), (v_part_lo, first), (hw_part_lo, second), (root0, first),
                        (x1_part_lo, first), (double_x1, first))

            all_graphs(pool, steps)


SET_SCORE = 3 + 6 + 2
SET_FIRST = SET_SCORE + 2
SET_BW = SET_FIRST + 6 + 2 + 1
SET_END = SET_BW + 4 + 2
SET_ACT_END = 7


_INS = ["x", "adj", "L0_gnn_Wv", "L0_gnn_bv", "L0_gnn_aw", "L0_gnn_ab", "L0_gnn_Wk", "L0_gnn_bk",
        "L1_gnn_W1", "L1_gnn_b1", "L1_gnn_gamma", "L1_gnn_beta", "L1_gnn_W2", "L1_gnn_b2"]
_OUT = ((16, 512, 256), "float32")


def kernel(**inputs):
    import numpy as _np
    import concourse.bacc as _bacc
    from concourse import mybir as _mybir
    from concourse.bass_utils import run_bass_kernel_spmd as _run

    nc = _bacc.Bacc("TRN2", target_bir_lowering=False, num_devices=1)
    arrays, args = {}, []
    for name in _INS:
        a = _np.ascontiguousarray(inputs[name])
        arrays[f"in_{name}"] = a
        args.append(nc.dram_tensor(f"in_{name}", a.shape, _mybir.dt.from_np(a.dtype), kind="ExternalInput").ap())
    shape, dtype = _OUT
    args.append(nc.dram_tensor("out_0", shape, _mybir.dt.from_np(_np.dtype(dtype)), kind="ExternalOutput").ap())
    gnn_resnorm(nc, *args)
    return _run(nc, [arrays], core_ids=[0]).results[0]["out_0"]
```

```python
from contextlib import ExitStack

import concourse.bass as bass
from concourse import mybir

P = 128
F32 = mybir.dt.float32
F32R = mybir.dt.float32r
ALU = mybir.AluOpType
ACT = mybir.ActivationFunctionType
AX_X = mybir.AxisListType.X
DMA = 16


class Count:

    def __init__(self, sem, per, unit=1):
        self.sem, self.per, self.unit = sem, per, unit

    def value(self, n, k):
        return (n * self.per + k) * self.unit


class Graph:

    def __init__(self, n, parity):
        self.n, self.parity = n, parity


def wait(engine, count, n, k):
    value = count.value(n, k)
    if isinstance(value, int) and value <= 0:
        return
    engine.wait_ge(count.sem, value)


def gnn_resnorm(nc, x, adj, Wv, bv, aw, ab, Wk, bk, W1, b1, gamma, beta, W2, b2, out):
    G, N, D = x.shape
    HID = W1.shape[0]
    NB, DB, HB = N // P, D // P, HID // P
    EPS = 1e-5
    NEG = 0.2
    DA = D + 2
    LN_STEPS = 2 * NB + 2
    assert N == 512 and HID == 512 and D == 256 and G % 2 == 0 and G >= 6

    with ExitStack() as ctx:
        def sb(name, shape, dt=F32):
            return ctx.enter_context(nc.sbuf_tensor(name, shape, dt))

        def sem(name):
            return ctx.enter_context(nc.semaphore(name))

        def per_graph(name, per, unit=1):
            return Count(sem(name), per, unit)

        ident = sb("ident", [P, P])
        wa_hi, wa_lo = (sb(f"wa_{s}", [P, DB, DA], F32R) for s in ("hi", "lo"))
        wb_hi, wb_lo = (sb(f"wb_{s}", [P, DB, 2 * D], F32R) for s in ("hi", "lo"))
        w1t_hi, w1t_lo = (sb(f"w1t_{s}", [P, DB, HID], F32R) for s in ("hi", "lo"))
        w2c_hi, w2c_lo = (sb(f"w2c_{s}", [P, HB, D], F32R) for s in ("hi", "lo"))
        score_const = sb("score_const", [P, 2])
        bk_row = sb("bk_row", [P, D])
        b1_row = sb("b1_row", [P, HID])
        b2_row = sb("b2_row", [P, D])
        bw_row = sb("bw_row", [P, D])
        minus_half = sb("minus_half", [P, NB])
        small = sb("small", [P, 16])

        x_in = [sb(f"x_in{i}", [P, NB, D]) for i in range(2)]
        adj_in = sb("adj_in", [P, NB, N])
        w_row = sb("w_row", [P, N])
        xt_hi, xt_lo = (sb(f"xt_{s}", [P, DB, N], F32R) for s in ("hi", "lo"))
        y2_hi = sb("y2_hi", [P, NB, DA], F32R)
        y2_lo = sb("y2_lo", [P, NB, D], F32R)
        y10 = sb("y10", [P, NB, 2 * D])
        scores = sb("scores", [P, NB, 2])
        score8, score2 = sb("score8", [P, NB]), sb("score2", [P, NB])
        si_rep = sb("si_rep", [P, NB, P])
        si_row, si_row2 = sb("si_row", [P, N]), sb("si_row2", [P, N])
        alpha = sb("alpha", [P, NB, N])
        al_hi, al_lo = (sb(f"al_{s}", [P, NB, N], F32R) for s in ("hi", "lo"))
        v_hi, v_lo = (sb(f"v_{s}", [P, NB, D], F32R) for s in ("hi", "lo"))
        rowsum, rowinv = sb("rowsum", [P, NB]), sb("rowinv", [P, NB])
        stats0, moments0 = sb("stats0", [P, NB, 6]), sb("moments0", [P, NB, 2])
        var0, rstd0 = sb("var0", [P, NB]), sb("rstd0", [P, NB])

        x1 = sb("x1", [P, NB, D])
        x1_hi = sb("x1_hi", [P, NB, D], F32R)
        x1_lo = sb("x1_lo", [P, NB, D], F32R)
        x1_b2 = sb("x1_b2", [P, NB, D])
        inc = sb("inc", [P, NB, N], F32R)
        inc_t = [sb(f"inc_t{i}", [P, NB, N], F32R) for i in range(2)]
        deg = sb("deg", [P, 4, NB])
        dn = [sb(f"dn{i}", [P, NB]) for i in range(2)]

        be_count, be_max = sb("be_count", [P, NB]), sb("be_max", [P, NB])
        be = [sb(f"be{i}", [P, NB]) for i in range(2)]
        sign = sb("sign", [P, 2, N])
        m_hi, m_lo = (sb(f"m_{s}", [P, NB, D], F32R) for s in ("hi", "lo"))
        ut_hi, ut_lo = (sb(f"ut_{s}", [P, DB, N], F32R) for s in ("hi", "lo"))
        h = sb("h", [P, NB, HID])
        stats1, moments1 = sb("stats1", [P, NB, 6]), sb("moments1", [P, NB, 2])
        var1, rstd1 = sb("var1", [P, NB]), sb("rstd1", [P, NB])
        ht_hi, ht_lo = (sb(f"ht_{s}", [P, HB, N], F32R) for s in ("hi", "lo"))
        hw = sb("hw", [P, NB, D])
        hw_hi = ut_hi[:, :, :].rearrange("p d (a c) -> p (d a) c", c=D)
        hw_lo = ut_lo[:, :, :].rearrange("p d (a c) -> p (d a) c", c=D)
        y = sb("y", [P, NB, D])
        stats2, moments2 = sb("stats2", [P, NB, 6]), sb("moments2", [P, NB, 2])
        var2, rstd2, shift2 = sb("var2", [P, NB]), sb("rstd2", [P, NB]), sb("shift2", [P, NB])

        pb = [ctx.enter_context(nc.psum_tensor(f"pb{i}", [P, 512], F32)) for i in range(4)]
        pc = [ctx.enter_context(nc.psum_tensor(f"pc{i}", [P, 512], F32)) for i in range(4)]
        bank_xt = [pb[0], pb[1]]
        bank_a = [pb[2], pb[3], pb[0], pb[1]]
        bank_si = pb[2]
        bank_adj = [pb[0], pb[1], pb[3], pb[2]]
        bank_l0 = pb
        M_ORDER = (2, 3, 0, 1)
        bank_l1 = [pc[2], pc[3], pc[0], pc[1]]

        rest_done = sem("rest_done")
        ident_done = sem("ident_done")
        score_in, wa_in, wb_in, w1_in, w2_in, rows_in = (
            sem(s) for s in ("score_in", "wa_in", "wb_in", "w1_in", "w2_in", "rows_in"))
        set_dve = sem("set_dve")
        set_act = sem("set_act")
        set_pe = sem("set_pe")
        set_pool = sem("set_pool")
        x_loaded, adj_loaded, w_loaded = (
            per_graph(s, 1, DMA) for s in ("x_loaded", "adj_loaded", "w_loaded"))
        stored = per_graph("stored", 2, DMA)
        xt_ps, proj_a, si_ps, adj_t, proj_b, hop1, hop2 = (
            per_graph(s, k) for s, k in (("xt_ps", DB), ("proj_a", NB), ("si_ps", 1), ("adj_t", NB),
                                         ("proj_b", NB), ("hop1", NB), ("hop2", NB)))
        xt_hi_done, xt_lo_done = per_graph("xt_hi_done", DB), per_graph("xt_lo_done", DB)
        y2_hi_done, y2_lo_done = per_graph("y2_hi_done", NB), per_graph("y2_lo_done", NB)
        scores_done, score_cols, si_rep_done = (
            per_graph("scores_done", NB), per_graph("score_cols", 2), per_graph("si_rep_done", 1))
        si_rows = per_graph("si_rows", 2)
        sign_done, inc_t_done = per_graph("sign_done", NB), per_graph("inc_t_done", NB)
        lrelu_done, exp_done, alpha_done = (
            per_graph(s, NB) for s in ("lrelu_done", "exp_done", "alpha_done"))
        al_hi_done, al_lo_done = per_graph("al_hi_done", NB), per_graph("al_lo_done", NB)
        y10_done, bias_done = per_graph("y10_done", NB), per_graph("bias_done", 1)
        rowinv_done = per_graph("rowinv_done", 2 * NB)
        v_done, v_hi_done, v_lo_done = (
            per_graph("v_done", NB), per_graph("v_hi_done", NB), per_graph("v_lo_done", NB))
        hop2_read, res_done = per_graph("hop2_read", NB), per_graph("res_done", NB)
        ln0 = per_graph("ln0", LN_STEPS)
        rstd0_done = per_graph("rstd0_done", 1)
        x1_done, x1_hi_done, x1_lo_done, x1_b2_done = (
            per_graph(s, k) for s, k in (("x1_done", NB), ("x1_hi_done", NB), ("x1_lo_done", NB),
                                         ("x1_b2_done", 2)))
        inc_done, dn_sum, dn_step = per_graph("inc_done", 1), per_graph("dn_sum", NB), per_graph("dn_step", 5)
        m_ps, ut_ps, z_ps, ht_ps, hw_ps, m2_ps, y_ps = (
            per_graph(s, k) for s, k in (("m_ps", NB), ("ut_ps", DB), ("z_ps", NB), ("ht_ps", HB),
                                         ("hw_ps", NB), ("m2_ps", NB), ("y_ps", NB)))
        be_done = per_graph("be_done", 2)
        m_hi_done, m_lo_done = per_graph("m_hi_done", NB), per_graph("m_lo_done", NB)
        ut_hi_done, ut_lo_done = per_graph("ut_hi_done", DB), per_graph("ut_lo_done", DB)
        z_done, h_done, ln1 = per_graph("z_done", NB), per_graph("h_done", NB), per_graph("ln1", LN_STEPS)
        rstd1_done = per_graph("rstd1_done", 1)
        ht_hi_done, ht_lo_done = per_graph("ht_hi_done", HB), per_graph("ht_lo_done", HB)
        hw_done, hw_hi_done, hw_lo_done = (
            per_graph("hw_done", NB), per_graph("hw_hi_done", NB), per_graph("hw_lo_done", NB))
        m2_hi_done, m2_lo_done = per_graph("m2_hi_done", NB), per_graph("m2_lo_done", NB)
        shift2_done = per_graph("shift2_done", 1)
        y_done, ln2, rstd2_done, out_done = (
            per_graph("y_done", NB), per_graph("ln2", LN_STEPS), per_graph("rstd2_done", 1),
            per_graph("out_done", NB))

        wa_f = alpha[:, 0:2, :].rearrange("p a n -> p (a n)")[:, 0:DB * DA].rearrange(
            "p (k c) -> p k c", c=DA)
        wb_f = alpha[:, 2:4, :]
        w1_f = x1[:, :, :]
        w2_f = y[:, :, :].rearrange("p a c -> p (a c)").rearrange("p (o k) -> p o k", k=HID)
        w2_g = hw[:, :, :].rearrange("p a c -> p (a c)").rearrange("p (o k) -> p o k", k=HID)
        wv_f = h[:, 0, :].rearrange("p (k c) -> p k c", c=D)
        aw_f = h[:, 1, :]
        bv_f = h[:, 2, 0:D]
        ab_f = h[:, 2, D:D + 1]
        gamma_f = h[:, 3, :]
        beta_f = x_in[1][:, 0:2, :].rearrange("p a c -> p (a c)")
        bk_f = x1_b2[:, 0:3, :]
        bw_rep = h[:, 0, 0:DB * P].rearrange("p (o c) -> p o c", c=P)
        left_over = si_rep[:, :, :].rearrange("p a c -> p (a c)")

        def f32(ap):
            return ap.bitcast(F32)

        block = ctx.enter_context(nc.Block())

        def all_graphs(engine, steps):
            def run(*graphs):
                for step, g, *rest in steps(*graphs):
                    if g is not None:
                        step(g, *rest)

            def around(n, parity):
                return [Graph(n + k, (parity + k) % 2) for k in (-1, 0, 1, 2)]

            run(None, None, None, Graph(0, 0))
            run(None, None, Graph(0, 0), Graph(1, 1))
            run(None, *around(0, 0)[1:])
            with engine.Fori(0, (G - 4) // 2) as i:
                run(*around(i * 2 + 1, 1))
                run(*around(i * 2 + 2, 0))
            run(*around(G - 3, 1))
            run(*around(G - 2, 0)[:3], None)
            run(*around(G - 1, 1)[:2], None, None)
            run(Graph(G - 1, 1), None, None, None)

        def once(g):
            return g if g is not None and isinstance(g.n, int) and g.n == 0 else None

        def last(g):
            return g if g is not None and isinstance(g.n, int) and g.n == G - 1 else None

        def before_last(g):
            return None if last(g) else g

        @block.sync
        def _(sp):
            def across(row):
                return row.partition_broadcast(P)

            def load_x(n, parity):
                sp.dma_start(x_in[parity][:, :, :],
                             x[bass.ds(n, 1), :, :].rearrange("g (r p) c -> p (g r) c", p=P)
                             ).then_inc(x_loaded.sem, DMA)

            load_x(0, 0)
            sp.dma_start(wv_f, Wv.rearrange("(k p) c -> p k c", p=P)).then_inc(score_in, DMA)
            sp.dma_start(aw_f, across(aw.rearrange("a b -> (a b)"))).then_inc(score_in, DMA)
            sp.dma_start(bv_f, across(bv)).then_inc(score_in, DMA)
            sp.dma_start(ab_f, across(ab)).then_inc(score_in, DMA)

            def load_adj(n):
                sp.dma_start(adj_in[:, :, :],
                             adj[bass.ds(n, 1), :, :].rearrange("g (r p) c -> p (g r) c", p=P)
                             ).then_inc(adj_loaded.sem, DMA)
                sp.dma_start(w_row[:, :], adj[bass.ds(n, 1), 0:1, :].rearrange("g a c -> (g a c)")
                             .partition_broadcast(P)).then_inc(w_loaded.sem, DMA)

            sp.dma_start(wa_f[:, :, 0:D], Wk[2].rearrange("(k p) c -> p k c", p=P)).then_inc(wa_in, DMA)
            sp.dma_start(wb_f[:, :, 0:D], Wk[1].rearrange("(k p) c -> p k c", p=P)).then_inc(wb_in, DMA)
            sp.dma_start(wb_f[:, :, D:2 * D], Wk[0].rearrange("(k p) c -> p k c", p=P)).then_inc(wb_in, DMA)
            load_adj(0)
            sp.dma_start(w1_f, W1.rearrange("(k p) c -> p k c", p=P)).then_inc(w1_in, DMA)
            sp.dma_start(w2_f, W2.rearrange("(k p) c -> p k c", p=P)).then_inc(w2_in, DMA)
            sp.dma_start(gamma_f, across(gamma)).then_inc(w2_in, DMA)
            sp.dma_start(beta_f, across(beta)).then_inc(w2_in, DMA)
            sp.dma_start(bk_f, across(bk.rearrange("a c -> (a c)")).rearrange("p (a c) -> p a c", c=D)
                         ).then_inc(rows_in, DMA)
            sp.dma_start(b1_row[:, :], across(b1)).then_inc(rows_in, DMA)
            sp.dma_start(b2_row[:, :], across(b2)).then_inc(rows_in, DMA)

            def adj_of(g):
                wait(sp, inc_done, g.n - 1, 1)
                wait(sp, dn_sum, g.n - 1, NB)
                load_adj(g.n)

            def x_after(g):
                wait(sp, x_loaded, g.n, 1)
                wait(sp, res_done, g.n - 1, NB)
                load_x(g.n + 1, 1 - g.parity)

            def store(n):
                for s in range(2):
                    if s == 1 and isinstance(n, int) and n == G - 1:
                        sp.wait_ge(rest_done, NB // 2)
                    else:
                        wait(sp, out_done, n, 2 * s + 2)
                    sp.dma_start(out[bass.ds(n, 1), s * N // 2:(s + 1) * N // 2, :]
                                 .rearrange("g (r p) c -> p (g r) c", p=P),
                                 y[:, 2 * s:2 * s + 2, :]).then_inc(stored.sem, DMA)

            sp.wait_ge(set_dve, SET_BW)
            x_after(Graph(0, 0))
            adj_of(Graph(1, 1))
            x_after(Graph(1, 1))
            adj_of(Graph(2, 0))
            x_after(Graph(2, 0))
            with sp.Fori(0, (G - 4) // 2) as i:
                for k in range(2):
                    g = Graph(i * 2 + 3 + k, 1 - k)
                    store(i * 2 + k)
                    adj_of(g)
                    x_after(g)
            store(G - 4)
            adj_of(Graph(G - 1, 1))
            for n in range(G - 3, G):
                store(n)
            wait(sp, stored, G - 1, 2)

        @block.tensor
        def _(pe):
            def product(bank, blocks, signal, ready=None, start=True, stop=True):
                for k, terms in enumerate(blocks):
                    if ready:
                        ready(k)
                    for t, (left, right) in enumerate(terms):
                        last = nc.tensor.matmul(
                            bank[:, 0:right.shape[-1]], left, right, start=(start and k == 0 and t == 0),
                            stop=(stop and k == len(blocks) - 1 and t == len(terms) - 1))
                if stop:
                    last.then_inc(signal, 1)

            def transposes(bank, blocks, signal):
                for t, block_in in enumerate(blocks):
                    last = nc.tensor.transpose(bank[:, t * P:(t + 1) * P], block_in, ident[:, :])
                last.then_inc(signal, 1)

            def cols(ap, k, b):
                return ap[:, k, b * P:(b + 1) * P]

            def transpose_x(g):
                xs = x_in[g.parity]
                wait(pe, x_loaded, g.n, 1)
                for k in range(DB):
                    wait(pe, hop2_read, g.n - 1, 1 + k)
                    transposes(bank_xt[k], [cols(xs, r, k) for r in range(NB)], xt_ps.sem)

            def project_a(g):
                wait(pe, xt_hi_done, g.n, DB)
                wait(pe, xt_lo_done, g.n, DB)
                if once(g):
                    pe.wait_ge(set_dve, SET_WA)
                for r in range(NB):
                    if r < 2:
                        wait(pe, hop2_read, g.n - 1, 3 + r)
                    product(bank_a[r], [[(cols(a, k, r), b[:, k, :])
                                         for a, b in ((xt_hi, wa_hi), (xt_hi, wa_lo), (xt_lo, wa_hi))]
                                        for k in range(DB)], proj_a.sem)

            def transpose_si(g):
                wait(pe, si_rep_done, g.n, 1)
                wait(pe, y2_lo_done, g.n, 1)
                transposes(bank_si, [si_rep[:, r, :] for r in range(NB)], si_ps.sem)

            def transpose_adj(g, *blocks):
                wait(pe, adj_loaded, g.n, 1)
                for j in blocks:
                    if j < NB - 1:
                        wait(pe, y2_lo_done, g.n, bank_a.index(bank_adj[j]) + 1)
                        wait(pe, scores_done, g.n, bank_a.index(bank_adj[j]) + 1)
                    else:
                        wait(pe, si_rows, g.n, 2)
                    transposes(bank_adj[j], [cols(adj_in, r, j) for r in range(NB)], adj_t.sem)

            def project_b(g):
                if once(g):
                    pe.wait_ge(set_dve, SET_WB)
                for r in range(NB):
                    wait(pe, alpha_done, g.n, bank_adj.index(bank_l0[r]) + 1)
                    product(bank_l0[r], [[(cols(a, k, r), b[:, k, :])
                                          for a, b in ((xt_hi, wb_hi), (xt_hi, wb_lo), (xt_lo, wb_hi))]
                                         for k in range(DB)], proj_b.sem)

            def hop_one(g):
                def split(j):
                    wait(pe, al_hi_done, g.n, j + 1)
                    wait(pe, al_lo_done, g.n, j + 1)

                for r in range(NB):
                    wait(pe, y10_done, g.n, r + 1)
                    product(bank_l0[r], [[(cols(a, j, r), b[:, j, :])
                                          for a, b in ((al_hi, y2_hi), (al_hi, y2_lo), (al_lo, y2_hi))]
                                         for j in range(NB)], hop1.sem, split if r == 0 else None)

            def hop_two(g):
                def split(j):
                    wait(pe, v_hi_done, g.n, j + 1)
                    wait(pe, v_lo_done, g.n, j + 1)

                for r in range(NB):
                    product(bank_l0[r], [[(cols(a, j, r), b[:, j, :])
                                          for a, b in ((al_hi, v_hi), (al_hi, v_lo), (al_lo, v_hi))]
                                         for j in range(NB)], hop2.sem, split if r == 0 else None)

            def edges_of_x(g):
                def split(c):
                    wait(pe, x1_hi_done, g.n, c + 1)
                    wait(pe, x1_lo_done, g.n, c + 1)

                if once(g):
                    pe.wait_ge(set_dve, SET_END)
                    pe.wait_ge(set_act, SET_ACT_END)
                wait(pe, inc_done, g.n, 1)
                for t, e in enumerate(M_ORDER):
                    wait(pe, y_done, g.n - 1, t + 1)
                    product(pc[e], [[(cols(inc, c, e), b[:, c, :]) for b in (x1_hi, x1_lo)]
                                    for c in range(NB)], m_ps.sem, split if t == 0 else None)

            def nodes_of_m(g):
                def split(t):
                    wait(pe, m_hi_done, g.n, max(t, M_ORDER.index(0)) + 1)
                    wait(pe, m_lo_done, g.n, max(t, M_ORDER.index(0)) + 1)

                wait(pe, inc_t_done, g.n, NB)
                for d in range(DB):
                    product(pc[d], [[(cols(a, e, d), inc_t[g.parity][:, e, :]) for a in (m_hi, m_lo)]
                                    for e in M_ORDER], ut_ps.sem, split if d == 0 else None)

            def hidden(g):
                def terms(c, d):
                    return [(cols(a, d, c), b[:, d, :])
                            for a, b in ((ut_hi, w1t_hi), (ut_hi, w1t_lo), (ut_lo, w1t_hi))]

                for d in range(DB):
                    wait(pe, ut_hi_done, g.n, d + 1)
                    wait(pe, ut_lo_done, g.n, d + 1)
                    for c in range(2):
                        if d == 0:
                            product(bank_l1[c], [terms(c, d)], None, stop=False)
                        else:
                            product(bank_l1[c], [terms(c, d)], z_ps.sem, start=False)
                for c in range(2, NB):
                    product(bank_l1[c], [terms(c, d) for d in range(DB)], z_ps.sem)

            def transpose_h(g):
                wait(pe, h_done, g.n, NB)
                for k in range(HB):
                    wait(pe, z_done, g.n, k + 1)
                    transposes(bank_l1[k], [cols(h, c, k) for c in range(NB)], ht_ps.sem)

            def hidden_out(g):
                def split(k):
                    wait(pe, ht_hi_done, g.n, k + 1)
                    wait(pe, ht_lo_done, g.n, k + 1)

                for c in range(NB):
                    product(bank_l1[c], [[(cols(a, k, c), b[:, k, :])
                                          for a, b in ((ht_hi, w2c_hi), (ht_hi, w2c_lo), (ht_lo, w2c_hi))]
                                         for k in range(HB)], hw_ps.sem, split if c == 0 else None)

            def edges_of_hw(g):
                def split(c):
                    wait(pe, hw_hi_done, g.n, c + 1)
                    wait(pe, hw_lo_done, g.n, c + 1)

                for e in range(NB):
                    product(bank_l1[e], [[(cols(inc, c, e), b[:, c, :]) for b in (hw_hi, hw_lo)]
                                         for c in range(NB)], m2_ps.sem, split if e == 0 else None)

            def nodes_of_m2(g):
                def split(e):
                    wait(pe, m2_hi_done, g.n, e + 1)
                    wait(pe, m2_lo_done, g.n, e + 1)

                for c in range(NB):
                    product(bank_l1[c], [[(cols(inc_t[g.parity], e, c), b[:, e, :]) for b in (m_hi, m_lo)]
                                         for e in range(NB)], y_ps.sem, split if c == 0 else None)

            def transpose_w1(g):
                pe.wait_ge(w1_in, DMA)
                for d in range(DB):
                    transposes(pc[d], [cols(w1_f, k, d) for k in range(HB)], set_pe)

            def transpose_w2(g):
                pe.wait_ge(set_dve, SET_BW)
                for b in range(2):
                    transposes(pc[2 + b], [w2_g[:, o, k * P:(k + 1) * P] for k in (2 * b, 2 * b + 1)
                                           for o in range(DB)], set_pe)

            def beta_row(g):
                pe.wait_ge(set_dve, SET_BW + 1)
                transposes(pc[0], [bw_rep[:, o, :] for o in range(DB)], set_pe)

            def keep_warm(g, products):
                for _ in range(products):
                    nc.tensor.transpose(pc[3][:, 0:P], ident[:, :], ident[:, :])

            pe.wait_ge(ident_done, 2)

            def steps(done, second, first, after):
                if once(after):
                    return ((keep_warm, after, 12), (transpose_x, after), (keep_warm, after, 20),
                            (project_a, after))
                if once(first):
                    return ((transpose_si, first), (transpose_adj, first, 0, 1, 2, 3), (keep_warm, first, 20),
                            (project_b, first), (transpose_w1, first), (hop_one, first),
                            (transpose_w2, first), (hop_two, first), (transpose_x, after),
                            (beta_row, first), (project_a, after))
                return ((edges_of_x, second), (transpose_si, first), (transpose_adj, first, 0, 1),
                        (nodes_of_m, second), (transpose_adj, first, 2, 3),
                        (hidden, second), (project_b, first), (transpose_h, second), (hop_one, first),
                        (hidden_out, second), (hop_two, first), (transpose_x, after),
                        (edges_of_hw, second), (project_a, after), (nodes_of_m2, second))

            all_graphs(pe, steps)

        @block.scalar
        def _(act):
            def copy(dst, src, signal, scale=1.0):
                nc.scalar.activation(dst, src, ACT.Copy, scale=scale).then_inc(signal, 1)

            def x_hi(g):
                for k in range(DB):
                    wait(act, xt_ps, g.n, k + 1)
                    copy(xt_hi[:, k, :], bank_xt[k][:, :], xt_hi_done.sem)

            def proj_a_hi(g):
                for r in range(NB):
                    wait(act, proj_a, g.n, r + 1)
                    copy(y2_hi[:, r, 0:D], bank_a[r][:, 0:D], y2_hi_done.sem)

            def score_rows(g):
                wait(act, si_ps, g.n, 1)
                wait(act, lrelu_done, g.n - 1, NB)
                copy(si_row[:, :], bank_si[:, :], si_rows.sem)
                copy(si_row2[:, :], bank_si[:, :], si_rows.sem, scale=NEG)

            def exps(g, *blocks):
                for j in blocks:
                    wait(act, lrelu_done, g.n, j + 1)
                    nc.scalar.activation(alpha[:, j, :], alpha[:, j, :], ACT.Exp,
                                         bias=score2[:, j:j + 1]).then_inc(exp_done.sem, 1)

            def incidence_t(g, *blocks):
                for j in blocks:
                    wait(act, adj_t, g.n, j + 1)
                    wait(act, inc_t_done, g.n, j - 1)
                    nc.scalar.activation(sign[:, j % 2, :], bank_adj[j][:, :], ACT.Sign
                                         ).then_inc(sign_done.sem, 1)
                    wait(act, sign_done, g.n, j + 1)
                    if j == 0:
                        wait(act, be_done, g.n - 1, 1)
                    nc.scalar.activation(inc_t[g.parity][:, j, :], sign[:, j % 2, :], ACT.Square,
                                         accum_out=be_count[:, j:j + 1]).then_inc(inc_t_done.sem, 1)

            def alpha_hi(g):
                for j in range(NB):
                    wait(act, alpha_done, g.n, j + 1)
                    copy(al_hi[:, j, :], alpha[:, j, :], al_hi_done.sem)

            def proj_b_out(g):
                for r in range(NB):
                    wait(act, proj_b, g.n, r + 1)
                    if r == 0:
                        wait(act, x1_done, g.n - 1, NB)
                    copy(y10[:, r, :], bank_l0[r][:, :], y10_done.sem)

            def v_part_hi(g):
                for r in range(NB):
                    wait(act, v_done, g.n, r + 1)
                    copy(v_hi[:, r, :], y10[:, r, 0:D], v_hi_done.sem)

            def x1_part_hi(g):
                wait(act, m_ps, g.n - 1, NB)
                for r in range(NB):
                    wait(act, x1_done, g.n, r + 1)
                    copy(x1_hi[:, r, :], x1[:, r, :], x1_hi_done.sem)

            def m_part_hi(g):
                for t, e in enumerate(M_ORDER):
                    wait(act, m_ps, g.n, t + 1)
                    wait(act, be_done, g.n, 2)
                    copy(m_hi[:, e, :], pc[e][:, 0:D], m_hi_done.sem, scale=be[g.parity][:, e:e + 1])

            def ut_part_hi(g, d):
                wait(act, ut_ps, g.n, d + 1)
                copy(ut_hi[:, d, :], pc[d][:, :], ut_hi_done.sem)

            def result(g):
                wait(act, shift2_done, g.n, 1)
                for c in range(NB // 2 if last(g) else NB):
                    nc.scalar.activation(y[:, c, :], y[:, c, :], ACT.Identity, bias=shift2[:, c:c + 1],
                                         scale=rstd2[:, c:c + 1]).then_inc(out_done.sem, 1)

            def relu_h(g):
                for c in range(NB):
                    wait(act, z_done, g.n, c + 1)
                    nc.scalar.activation(h[:, c, :], h[:, c, :], ACT.Relu).then_inc(h_done.sem, 1)

            def ht_part_hi(g):
                for k in range(HB):
                    wait(act, ht_ps, g.n, k + 1)
                    copy(ht_hi[:, k, :], bank_l1[k][:, :], ht_hi_done.sem)

            def hw_part_hi(g):
                for c in range(NB):
                    wait(act, hw_done, g.n, c + 1)
                    copy(hw_hi[:, c, :], hw[:, c, :], hw_hi_done.sem)

            def m2_part_hi(g):
                for e in range(NB):
                    wait(act, m2_ps, g.n, e + 1)
                    copy(m_hi[:, e, :], bank_l1[e][:, 0:D], m2_hi_done.sem, scale=be[g.parity][:, e:e + 1])

            def first_weights(g):
                act.wait_ge(wa_in, DMA)
                copy(wa_hi[:, :, 0:D], wa_f[:, :, 0:D], set_act)
                act.wait_ge(set_dve, SET_COLS)
                copy(wa_hi[:, :, D:DA], wa_f[:, :, D:DA], set_act)
                act.wait_ge(wb_in, 2 * DMA)
                copy(wb_hi[:, :, :], wb_f, set_act)

            def w1_hi(g):
                for d in range(DB):
                    act.wait_ge(set_pe, d + 1)
                    copy(w1t_hi[:, d, :], pc[d][:, :], set_act)

            def w2_hi(g):
                for b in range(2):
                    act.wait_ge(set_pe, DB + b + 1)
                    copy(w2c_hi[:, 2 * b:2 * b + 2, :], pc[2 + b][:, :].rearrange("p (k c) -> p k c", c=D),
                         set_act)

            def beta_row(g):
                act.wait_ge(set_pe, DB + 3)
                copy(bw_row[:, :], pc[0][:, 0:D], set_act)

            def steps(done, second, first, after):
                if once(after):
                    return ((x_hi, after), (first_weights, after), (proj_a_hi, after))
                if once(first):
                    return ((score_rows, first), (incidence_t, first, 0), (exps, first, 0),
                            (incidence_t, first, 1), (exps, first, 1, 2, 3), (incidence_t, first, 2, 3),
                            (alpha_hi, first), (proj_b_out, first), (w1_hi, first), (v_part_hi, first),
                            (w2_hi, first), (x_hi, after), (beta_row, first), (x1_part_hi, first),
                            (proj_a_hi, after))
                return ((m_part_hi, second), (score_rows, first), (incidence_t, first, 0),
                        (ut_part_hi, second, 0), (exps, first, 0), (ut_part_hi, second, 1),
                        (incidence_t, first, 1), (exps, first, 1, 2, 3), (incidence_t, first, 2, 3),
                        (alpha_hi, first), (relu_h, second), (proj_b_out, first),
                        (ht_part_hi, second), (result, done), (v_part_hi, first),
                        (hw_part_hi, second), (x_hi, after), (m2_part_hi, second),
                        (x1_part_hi, first), (proj_a_hi, after))

            all_graphs(act, steps)

        @block.vector
        def _(dve):
            def lo_of(dst, src, hi, signal):
                nc.vector.tensor_tensor(dst, src, f32(hi), ALU.subtract).then_inc(signal, 1)

            def x_lo(g, k):
                wait(dve, xt_hi_done, g.n, k + 1)
                lo_of(xt_lo[:, k, :], bank_xt[k][:, :], xt_hi[:, k, :], xt_lo_done.sem)

            def proj_a_lo(g):
                for r in range(NB):
                    wait(dve, y2_hi_done, g.n, r + 1)
                    nc.vector.tensor_tensor(scores[:, r, :], bank_a[r][:, D:DA], score_const[:, :],
                                            ALU.add).then_inc(scores_done.sem, 1)
                    lo_of(y2_lo[:, r, :], bank_a[r][:, 0:D], y2_hi[:, r, 0:D], y2_lo_done.sem)
                wait(dve, scores_done, g.n, NB)
                nc.vector.tensor_copy(si_rep[:, :, :], scores[:, :, 1:2].to_broadcast([P, NB, P])
                                      ).then_inc(si_rep_done.sem, 1)
                nc.vector.tensor_scalar(score8[:, :], scores[:, :, 0], 1.0 - NEG, None, ALU.mult
                                        ).then_inc(score_cols.sem, 1)
                nc.vector.tensor_scalar(score2[:, :], scores[:, :, 0], NEG, None, ALU.mult
                                        ).then_inc(score_cols.sem, 1)

            def lrelu(g, *blocks):
                wait(dve, si_rows, g.n, 2)
                wait(dve, score_cols, g.n, 2)
                for j in blocks:
                    if j == 0:
                        wait(dve, dn_sum, g.n - 1, NB)
                    nc.vector.scalar_tensor_tensor(alpha[:, j, :], si_row[:, :], score8[:, j:j + 1],
                                                   si_row2[:, :], ALU.add, ALU.max).then_inc(lrelu_done.sem, 1)

            def alphas(g):
                for j in range(NB):
                    wait(dve, exp_done, g.n, j + 1)
                    wait(dve, sign_done, g.n, j + 1)
                    nc.vector.tensor_tensor(alpha[:, j, :], bank_adj[j][:, :], alpha[:, j, :],
                                            ALU.mult).then_inc(alpha_done.sem, 1)

            def first_hop(g, *rows):
                for r in rows:
                    wait(dve, hop1, g.n, r + 1)
                    nc.vector.tensor_scalar(rowsum[:, r:r + 1], bank_l0[r][:, D:D + 1], 1e-12, None,
                                            ALU.add).then_inc(rowinv_done.sem, 1)
                    wait(dve, rowinv_done, g.n, 2 * r + 1)
                    nc.vector.reciprocal(rowinv[:, r:r + 1], rowsum[:, r:r + 1]).then_inc(rowinv_done.sem, 1)
                    wait(dve, rowinv_done, g.n, 2 * r + 2)
                    nc.vector.scalar_tensor_tensor(y10[:, r, 0:D], bank_l0[r][:, 0:D], rowinv[:, r:r + 1],
                                                   y10[:, r, 0:D], ALU.mult, ALU.add).then_inc(v_done.sem, 1)

            def second_hop(g, *rows):
                wait(dve, bias_done, g.n, 1)
                for r in rows:
                    wait(dve, hop2, g.n, r + 1)
                    nc.vector.scalar_tensor_tensor(y10[:, r, D:2 * D], bank_l0[r][:, 0:D], rowinv[:, r:r + 1],
                                                   y10[:, r, D:2 * D], ALU.mult, ALU.add
                                                   ).then_inc(hop2_read.sem, 1)
                    wait(dve, hop2_read, g.n, r + 1)
                    nc.vector.scalar_tensor_tensor(y10[:, r, D:2 * D], y10[:, r, D:2 * D], 0.0,
                                                   x_in[g.parity][:, r, :], ALU.max, ALU.add
                                                   ).then_inc(res_done.sem, 1)
                    moments(g, y10[:, r, D:2 * D], res_done, stats0, moments0, var0, ln0, r)

            def moments(g, src, made, stats, mean_var, var, ln, r):
                wait(dve, made, g.n, r + 1)
                if r:
                    wait(dve, ln, g.n, max(1, 2 * (r - 1)))
                nc.vector.bn_stats(stats[:, r, :], src).then_inc(ln.sem, 1)
                if r:
                    nc.vector.bn_aggr(mean_var[:, r - 1, :], stats[:, r - 1, :]).then_inc(ln.sem, 1)
                if r == NB - 1:
                    wait(dve, ln, g.n, 2 * NB - 1)
                    nc.vector.tensor_scalar(var[:, 0:r], mean_var[:, 0:r, 1], EPS, None,
                                            ALU.add).then_inc(ln.sem, 1)
                    nc.vector.bn_aggr(mean_var[:, r, :], stats[:, r, :]).then_inc(ln.sem, 1)
                    wait(dve, ln, g.n, 2 * NB + 1)
                    nc.vector.tensor_scalar(var[:, r:r + 1], mean_var[:, r, 1:2], EPS, None,
                                            ALU.add).then_inc(ln.sem, 1)

            def normalise(g, dst, src, mean_var, rstd, done):
                for r in range(NB):
                    nc.vector.tensor_scalar(dst(r), src(r), mean_var[:, r, 0:1], rstd[:, r:r + 1],
                                            ALU.subtract, ALU.mult).then_inc(done.sem, 1)

            def x1_out(g):
                wait(dve, rstd0_done, g.n, 1)
                wait(dve, x1_b2_done, g.n - 1, 2)
                normalise(g, lambda r: x1[:, r, :], lambda r: y10[:, r, D:2 * D], moments0, rstd0, x1_done)

            def incidence(g):
                wait(dve, m2_ps, g.n - 1, NB)
                wait(dve, adj_loaded, g.n, 1)
                nc.vector.tensor_scalar(inc[:, :, :], adj_in[:, :, :], 0.0, None,
                                        ALU.not_equal).then_inc(inc_done.sem, 1)

            def degree_sums(g, r):
                wait(dve, adj_loaded, g.n, 1)
                wait(dve, w_loaded, g.n, 1)
                wait(dve, al_lo_done, g.n, NB)
                nc.vector.scalar_tensor_tensor(alpha[:, r, :], adj_in[:, r, :], 0.0, w_row[:, :],
                                               ALU.not_equal, ALU.mult,
                                               accum_out=deg[:, 0, r:r + 1]).then_inc(dn_sum.sem, 1)

            def degree_inverses(g):
                total, no_edge, safe, inverse = (deg[:, i, :] for i in range(4))
                wait(dve, dn_sum, g.n, NB)
                nc.vector.tensor_scalar(no_edge, total, 0.0, None, ALU.is_le).then_inc(dn_step.sem, 1)
                wait(dve, dn_step, g.n, 1)
                nc.vector.scalar_tensor_tensor(safe, total, 0.0, no_edge, ALU.max, ALU.add
                                               ).then_inc(dn_step.sem, 1)
                wait(dve, dn_step, g.n, 2)
                nc.vector.reciprocal(inverse, safe).then_inc(dn_step.sem, 1)
                wait(dve, dn_step, g.n, 3)
                nc.vector.tensor_tensor(safe, no_edge, inverse, ALU.mult).then_inc(dn_step.sem, 1)
                wait(dve, dn_step, g.n, 4)
                nc.vector.tensor_tensor(dn[g.parity][:, :], inverse, safe, ALU.subtract
                                        ).then_inc(dn_step.sem, 1)

            def edge_inverses(g):
                wait(dve, inc_t_done, g.n, NB)
                nc.vector.tensor_scalar(be_max[:, :], be_count[:, :], 1.0, None, ALU.max
                                        ).then_inc(be_done.sem, 1)
                wait(dve, be_done, g.n, 1)
                nc.vector.reciprocal(be[g.parity][:, :], be_max[:, :]).then_inc(be_done.sem, 1)

            def m_part_lo(g):
                for t, e in enumerate(M_ORDER):
                    wait(dve, m_hi_done, g.n, t + 1)
                    nc.vector.scalar_tensor_tensor(m_lo[:, e, :], pc[e][:, 0:D], be[g.parity][:, e:e + 1],
                                                   f32(m_hi[:, e, :]), ALU.mult, ALU.subtract
                                                   ).then_inc(m_lo_done.sem, 1)

            def ut_part_lo(g, d):
                wait(dve, ut_hi_done, g.n, d + 1)
                lo_of(ut_lo[:, d, :], pc[d][:, :], ut_hi[:, d, :], ut_lo_done.sem)

            def z_out(g):
                wait(dve, dn_step, g.n, 5)
                for c in range(NB):
                    wait(dve, z_ps, g.n, c + 1)
                    nc.vector.scalar_tensor_tensor(h[:, c, :], bank_l1[c][:, :], dn[g.parity][:, c:c + 1],
                                                   b1_row[:, :], ALU.mult, ALU.add).then_inc(z_done.sem, 1)

            def h_moments(g, *blocks):
                for c in blocks:
                    moments(g, h[:, c, :], h_done, stats1, moments1, var1, ln1, c)

            def ht_part_lo(g):
                for k in range(HB):
                    wait(dve, ht_hi_done, g.n, k + 1)
                    lo_of(ht_lo[:, k, :], bank_l1[k][:, :], ht_hi[:, k, :], ht_lo_done.sem)

            def hw_out(g, c):
                wait(dve, rstd1_done, g.n, 1)
                if once(g):
                    dve.wait_ge(set_act, SET_ACT_END)
                wait(dve, hw_ps, g.n, c + 1)
                nc.vector.scalar_tensor_tensor(hw[:, c, :], bank_l1[c][:, 0:D], rstd1[:, c:c + 1],
                                               bw_row[:, :], ALU.mult, ALU.add).then_inc(hw_done.sem, 1)

            def hw_part_lo(g, c):
                wait(dve, hw_hi_done, g.n, c + 1)
                lo_of(hw_lo[:, c, :], hw[:, c, :], hw_hi[:, c, :], hw_lo_done.sem)

            def m2_part_lo(g):
                for e in range(NB):
                    wait(dve, m2_hi_done, g.n, e + 1)
                    nc.vector.scalar_tensor_tensor(m_lo[:, e, :], bank_l1[e][:, 0:D], be[g.parity][:, e:e + 1],
                                                   f32(m_hi[:, e, :]), ALU.mult, ALU.subtract
                                                   ).then_inc(m2_lo_done.sem, 1)

            def y_out(g, c):
                if c == 0:
                    wait(dve, x1_b2_done, g.n, 2)
                    wait(dve, stored, g.n - 1, 2)
                wait(dve, y_ps, g.n, c + 1)
                nc.vector.scalar_tensor_tensor(y[:, c, :], bank_l1[c][:, 0:D], dn[g.parity][:, c:c + 1],
                                               x1_b2[:, c, :], ALU.mult, ALU.add
                                               ).then_inc(y_done.sem, 1)

            def y_moments(g, *blocks):
                for c in blocks:
                    moments(g, y[:, c, :], y_done, stats2, moments2, var2, ln2, c)

            def result_shift(g):
                wait(dve, rstd2_done, g.n, 1)
                wait(dve, out_done, g.n - 1, NB)
                nc.vector.scalar_tensor_tensor(shift2[:, :], moments2[:, :, 0], -1.0, rstd2[:, :],
                                               ALU.mult, ALU.mult).then_inc(shift2_done.sem, 1)

            def result_rest(g):
                for c in range(NB // 2, NB):
                    nc.vector.tensor_scalar(y[:, c, :], y[:, c, :], moments2[:, c, 0:1], rstd2[:, c:c + 1],
                                            ALU.subtract, ALU.mult).then_inc(rest_done, 1)

            steps_done = [0]

            def then(instruction, wait_for_it=False):
                steps_done[0] += 1
                instruction.then_inc(set_dve, 1)
                if wait_for_it:
                    dve.wait_ge(set_dve, steps_done[0])

            def dot(dst, a, b):
                then(nc.vector.scalar_tensor_tensor(left_over[:, 0:a.shape[-1]], a, 1.0, b, ALU.mult, ALU.mult,
                                                    accum_out=dst), True)

            then(nc.vector.memset(f32(y2_hi[:, :, D:D + 1]), 1.0))
            then(nc.vector.memset(f32(y2_hi[:, :, D + 1:DA]), 0.0))
            then(nc.vector.memset(minus_half[:, :], -0.5))

            def first_weights(g):
                dve.wait_ge(score_in, 4 * DMA)
                for s in range(2):
                    for k in range(DB):
                        dot(wa_f[:, k, D + s:D + s + 1], wv_f[:, k, :], aw_f[:, s * D:(s + 1) * D])
                assert steps_done[0] == SET_COLS
                for step, part in ((1, slice(0, D)), (2, slice(D, DA))):
                    dve.wait_ge(set_act, step)
                    then(nc.vector.tensor_tensor(wa_lo[:, :, part], wa_f[:, :, part],
                                                 f32(wa_hi[:, :, part]), ALU.subtract))
                assert steps_done[0] == SET_WA
                for s in range(2):
                    dot(small[:, s:s + 1], bv_f, aw_f[:, s * D:(s + 1) * D])
                then(nc.vector.tensor_copy(score_const[:, 0:1], small[:, 0:1]))
                then(nc.vector.tensor_tensor(score_const[:, 1:2], small[:, 1:2], ab_f, ALU.add), True)
                dve.wait_ge(set_act, 3)
                then(nc.vector.tensor_tensor(wb_lo[:, :, :], wb_f, f32(wb_hi[:, :, :]), ALU.subtract))
                assert steps_done[0] == SET_WB

            def second_weights(g):
                dve.wait_ge(rows_in, 3 * DMA)
                then(nc.vector.tensor_tensor(bk_row[:, :], bk_f[:, 0, :], bk_f[:, 1, :], ALU.add), True)
                then(nc.vector.tensor_tensor(bk_row[:, :], bk_row[:, :], bk_f[:, 2, :], ALU.add), True)
                assert steps_done[0] == SET_BIAS
                dve.wait_ge(w2_in, 3 * DMA)
                for o in range(DB):
                    then(nc.vector.scalar_tensor_tensor(w2_g[:, o, :], w2_f[:, o, :], 1.0, gamma_f, ALU.mult,
                                                        ALU.mult, accum_out=small[:, 4 + o:5 + o]), True)
                    then(nc.vector.tensor_scalar(small[:, 6 + o:7 + o], small[:, 4 + o:5 + o], 1.0 / HID,
                                                 None, ALU.mult), True)
                    then(nc.vector.tensor_scalar(w2_g[:, o, :], w2_g[:, o, :], small[:, 6 + o:7 + o], None,
                                                 ALU.subtract), True)
                for o in range(DB):
                    dot(small[:, 2 + o:3 + o], w2_f[:, o, :], beta_f)
                then(nc.vector.tensor_copy(bw_rep, small[:, 2:4].rearrange("p (a b) -> p a b", b=1)
                                           .to_broadcast([P, DB, P])))
                assert steps_done[0] == SET_BW

            def w1_lo(g):
                for d in range(DB):
                    dve.wait_ge(set_act, 4 + d)
                    then(nc.vector.tensor_tensor(w1t_lo[:, d, :], pc[d][:, :], f32(w1t_hi[:, d, :]),
                                                 ALU.subtract))

            def w2_lo(g):
                for b in range(2):
                    dve.wait_ge(set_act, 6 + b)
                    then(nc.vector.tensor_tensor(w2c_lo[:, 2 * b:2 * b + 2, :],
                                                 pc[2 + b][:, :].rearrange("p (k c) -> p k c", c=D),
                                                 f32(w2c_hi[:, 2 * b:2 * b + 2, :]), ALU.subtract))
                assert steps_done[0] == SET_END

            def steps(done, second, first, after):
                if once(after):
                    return ((x_lo, after, 0), (x_lo, after, 1), (first_weights, after), (proj_a_lo, after))
                if once(first):
                    return ((incidence, first), (lrelu, first, 0, 1, 2, 3), (alphas, first),
                            (edge_inverses, first), (second_weights, first), (w1_lo, first),
                            (first_hop, first, 0), (degree_sums, first, 0), (first_hop, first, 1),
                            (degree_sums, first, 1), (first_hop, first, 2), (degree_sums, first, 2),
                            (first_hop, first, 3), (degree_sums, first, 3), (w2_lo, first),
                            (second_hop, first, 0, 1, 2, 3), (x_lo, after, 0), (x_lo, after, 1),
                            (x1_out, first), (degree_inverses, first), (proj_a_lo, after))
                if last(second):
                    return ((m_part_lo, second), (ut_part_lo, second, 0), (ut_part_lo, second, 1),
                            (y_moments, done, 0, 1, 2, 3), (z_out, second), (h_moments, second, 0, 1),
                            (result_shift, done), (ht_part_lo, second), (h_moments, second, 2, 3),
                            (hw_out, second, 0), (hw_out, second, 1), (hw_part_lo, second, 0),
                            (hw_out, second, 2), (hw_part_lo, second, 1), (hw_out, second, 3),
                            (hw_part_lo, second, 2), (hw_part_lo, second, 3), (m2_part_lo, second),
                            (y_out, second, 0), (y_moments, second, 0), (y_out, second, 1),
                            (y_moments, second, 1), (y_out, second, 2), (y_moments, second, 2),
                            (y_out, second, 3), (y_moments, second, 3))
                if last(done):
                    return ((result_shift, done), (result_rest, done))
                return ((m_part_lo, second), (lrelu, first, 0, 1, 2),
                        (ut_part_lo, second, 0), (lrelu, first, 3), (ut_part_lo, second, 1), (y_moments, done, 0, 1, 2, 3),
                        (alphas, first), (edge_inverses, first),
                        (z_out, second), (h_moments, second, 0, 1), (result_shift, done),
                        (ht_part_lo, second), (h_moments, second, 2, 3), (first_hop, first, 0, 1, 2, 3), (hw_out, second, 0), (degree_sums, first, 0), (hw_out, second, 1),
                        (degree_sums, first, 1), (hw_out, second, 2), (degree_sums, first, 2),
                        (hw_out, second, 3), (degree_sums, first, 3), (degree_inverses, first),
                        (second_hop, first, 0, 1, 2), (x_lo, after, 0), (x_lo, after, 1),
                        (second_hop, first, 3), (m2_part_lo, second), (x1_out, first),
                        (incidence, first), (y_out, second, 0), (y_out, second, 1),
                        (proj_a_lo, after), (y_out, second, 2), (y_out, second, 3))

            all_graphs(dve, steps)

        @block.gpsimd
        def _(pool):
            def alpha_lo(g):
                for j in range(NB):
                    wait(pool, al_hi_done, g.n, j + 1)
                    if j == 0:
                        wait(pool, hop2, g.n - 1, NB)
                    nc.gpsimd.tensor_tensor(al_lo[:, j, :], alpha[:, j, :], f32(al_hi[:, j, :]),
                                            ALU.subtract).then_inc(al_lo_done.sem, 1)

            def v_part_lo(g):
                for r in range(NB):
                    wait(pool, v_hi_done, g.n, r + 1)
                    nc.gpsimd.tensor_tensor(v_lo[:, r, :], y10[:, r, 0:D], f32(v_hi[:, r, :]),
                                            ALU.subtract).then_inc(v_lo_done.sem, 1)

            def hw_part_lo(g):
                for c in range(NB):
                    wait(pool, hw_hi_done, g.n, c + 1)
                    nc.gpsimd.tensor_tensor(hw_lo[:, c, :], hw[:, c, :], f32(hw_hi[:, c, :]), ALU.subtract
                                            ).then_inc(hw_lo_done.sem, 1)

            def add_bias(g):
                wait(pool, y10_done, g.n, NB)
                if once(g):
                    pool.wait_ge(set_dve, SET_BIAS)
                nc.gpsimd.tensor_tensor(y10[:, :, D:2 * D], y10[:, :, D:2 * D],
                                        bk_row[:, :].rearrange("p (a c) -> p a c", a=1)
                                        .to_broadcast([P, NB, D]), ALU.add).then_inc(bias_done.sem, 1)

            def inverse_root(g, dst, var, ln, done):
                wait(pool, ln, g.n, LN_STEPS)
                nc.gpsimd.tensor_tensor(dst[:, :], var[:, :], minus_half[:, :], ALU.pow).then_inc(done.sem, 1)

            def root0(g):
                inverse_root(g, rstd0, var0, ln0, rstd0_done)

            def root1(g):
                inverse_root(g, rstd1, var1, ln1, rstd1_done)

            def root2(g):
                inverse_root(g, rstd2, var2, ln2, rstd2_done)

            def x1_part_lo(g):
                for r in range(NB):
                    wait(pool, x1_hi_done, g.n, r + 1)
                    nc.gpsimd.tensor_tensor(x1_lo[:, r, :], x1[:, r, :], f32(x1_hi[:, r, :]),
                                            ALU.subtract).then_inc(x1_lo_done.sem, 1)

            def double_x1(g):
                wait(pool, y_done, g.n - 1, NB)
                wait(pool, x1_done, g.n, NB)
                nc.gpsimd.tensor_tensor(x1_b2[:, :, :], x1[:, :, :], b2_row[:, :].rearrange(
                    "p (a c) -> p a c", a=1).to_broadcast([P, NB, D]), ALU.add).then_inc(x1_b2_done.sem, 1)
                wait(pool, x1_b2_done, g.n, 1)
                nc.gpsimd.tensor_tensor(x1_b2[:, :, :], x1_b2[:, :, :], x1[:, :, :], ALU.add
                                        ).then_inc(x1_b2_done.sem, 1)

            nc.gpsimd.memset(ident[:, :], 0.0).then_inc(ident_done, 1)
            pool.wait_ge(ident_done, 1)
            nc.gpsimd.affine_select(out=ident[:, :], in_=ident[:, :], compare_op=ALU.not_equal, fill=1.0,
                                    base=0, pattern=[[-1, P]], channel_multiplier=1).then_inc(ident_done, 1)

            def steps(done, second, first, after):
                return ((root2, done), (alpha_lo, first), (add_bias, first), (root1, second),
                        (v_part_lo, first), (hw_part_lo, before_last(second)), (root0, first),
                        (x1_part_lo, first), (double_x1, first))

            all_graphs(pool, steps)


SET_COLS = 3 + 4
SET_WA = SET_COLS + 2
SET_WB = SET_WA + 2 + 2 + 1
SET_BIAS = SET_WB + 2
SET_BW = SET_BIAS + 6 + 2 + 1
SET_END = SET_BW + 4
SET_ACT_END = 8


_INS = ["x", "adj", "L0_gnn_Wv", "L0_gnn_bv", "L0_gnn_aw", "L0_gnn_ab", "L0_gnn_Wk", "L0_gnn_bk",
        "L1_gnn_W1", "L1_gnn_b1", "L1_gnn_gamma", "L1_gnn_beta", "L1_gnn_W2", "L1_gnn_b2"]
_OUT = ((16, 512, 256), "float32")


def kernel(**inputs):
    import numpy as _np
    import concourse.bacc as _bacc
    from concourse import mybir as _mybir
    from concourse.bass_utils import run_bass_kernel_spmd as _run

    nc = _bacc.Bacc("TRN2", target_bir_lowering=False, num_devices=1)
    arrays, args = {}, []
    for name in _INS:
        a = _np.ascontiguousarray(inputs[name])
        arrays[f"in_{name}"] = a
        args.append(nc.dram_tensor(f"in_{name}", a.shape, _mybir.dt.from_np(a.dtype), kind="ExternalInput").ap())
    shape, dtype = _OUT
    args.append(nc.dram_tensor("out_0", shape, _mybir.dt.from_np(_np.dtype(dtype)), kind="ExternalOutput").ap())
    gnn_resnorm(nc, *args)
    return _run(nc, [arrays], core_ids=[0]).results[0]["out_0"]
```
